# Optimizing a Trainium2 kernel written in Bass

```python
import numpy as np
import jax
import jax.numpy as jnp

def _softmax(x, axis=-1):
    return jax.nn.softmax(x, axis=axis)

def _gelu(x):
    return jax.nn.gelu(x, approximate=True)

def _silu(x):
    return jax.nn.silu(x)

def _sigmoid(x):
    return jax.nn.sigmoid(x)

def _layernorm(x, axis=-1, eps=1e-05):
    m = jnp.mean(x, axis=axis, keepdims=True)
    v = jnp.var(x, axis=axis, keepdims=True)
    return (x - m) / jnp.sqrt(v + eps)

def _scatter_add(tgt, idx, src, axis=0):
    return tgt.at[idx].add(src)

def _segment_sum(src, seg, n):
    return jax.ops.segment_sum(src, seg, n)
kernel_name = 'mk_adaln_d1_jaxref_r8_18fe11'

def setup_inputs(seed: int=0):
    np.random.seed(seed)
    _w = jnp.asarray

    def _L0_attn_setup():
        import jax, jax.numpy as jnp
        import numpy as np
        MAX_DISTANCE = 10
        SCALE = 0.01

        def distance_bias(seq_len):
            idx = jnp.arange(seq_len, dtype=jnp.float32)
            d = jnp.abs(idx[None, :] - idx[:, None])
            return jnp.clip(d, 0.0, MAX_DISTANCE) * SCALE
        key = jax.random.key(seed)
        k1, k2 = jax.random.split(key)
        B, S, D_IN, D_OUT = (8, 256, 128, 128)
        x = jax.random.normal(k1, (B, S, D_IN), dtype=jnp.float32)
        W = jax.random.normal(k2, (D_IN, D_OUT), dtype=jnp.float32) * (1.0 / np.sqrt(D_IN))
        b = jnp.zeros((D_OUT,), dtype=jnp.float32)
        return {'x': x, 'W': W, 'b': b}
    _L0_attn_in = _L0_attn_setup()

    def _L0_ffn_setup():
        import jax, jax.numpy as jnp
        import numpy as np
        DIM = 128

        def _reference_tuple_inner(x, W_r, W_k, W_v, mu_r, mu_k):
            B, T, C = x.shape
            x_prev = jnp.concatenate([jnp.zeros((B, 1, C), x.dtype), x[:, :-1, :]], axis=1)
            xr = mu_r * x + (1.0 - mu_r) * x_prev
            xk = mu_k * x + (1.0 - mu_k) * x_prev
            r = jax.nn.sigmoid(jnp.einsum('btc,dc->btd', xr, W_r))
            k = jnp.einsum('btc,dc->btd', xk, W_k)
            k_act = jnp.square(jax.nn.relu(k))
            out = r * jnp.einsum('btc,dc->btd', k_act, W_v)
            new_state = x[:, -1, :]
            return (out, new_state)
        key = jax.random.key(seed)
        ks = jax.random.split(key, 6)
        B, T, C = (8, 256, DIM)
        x = jax.random.normal(ks[0], (B, T, C), dtype=jnp.float32)
        s = 1.0 / np.sqrt(C)
        W_r = jax.random.uniform(ks[1], (C, C), jnp.float32, -s, s)
        W_k = jax.random.uniform(ks[2], (C, C), jnp.float32, -s, s)
        W_v = jax.random.uniform(ks[3], (C, C), jnp.float32, -s, s)
        mu_r = jax.random.uniform(ks[4], (C,), jnp.float32)
        mu_k = jax.random.uniform(ks[5], (C,), jnp.float32)
        return {'x': x, 'W_r': W_r, 'W_k': W_k, 'W_v': W_v, 'mu_r': mu_r, 'mu_k': mu_k}
    _L0_ffn_in = _L0_ffn_setup()
    _L0_c = _w((lambda *s: np.random.randn(*s).astype(np.float32) * 0.05)(8, 128))
    _L0_wmod = _w((lambda *s: np.random.randn(*s).astype(np.float32) * 0.05)(128, 6 * 128) * 128 ** (-0.5))
    _d = {'L0_attn_x': _L0_attn_in['x'], 'L0_attn_W': _L0_attn_in['W'], 'L0_attn_b': _L0_attn_in['b'], 'L0_ffn_W_r': _L0_ffn_in['W_r'], 'L0_ffn_W_k': _L0_ffn_in['W_k'], 'L0_ffn_W_v': _L0_ffn_in['W_v'], 'L0_ffn_mu_r': _L0_ffn_in['mu_r'], 'L0_ffn_mu_k': _L0_ffn_in['mu_k'], 'L0_c': _L0_c, 'L0_wmod': _L0_wmod}
    _x0 = _d['L0_attn_x']
    _d['L0_attn_x'] = jax.random.normal(jax.random.fold_in(jax.random.key(seed), 1), (8, 512, 128), dtype=_x0.dtype)
    del _x0
    return _d

def reference(L0_attn_x, L0_attn_W, L0_attn_b, L0_ffn_W_r, L0_ffn_W_k, L0_ffn_W_v, L0_ffn_mu_r, L0_ffn_mu_k, L0_c, L0_wmod):

    def _L0_attn_ref(x, W, b):
        import jax, jax.numpy as jnp
        import numpy as np
        MAX_DISTANCE = 10
        SCALE = 0.01

        def distance_bias(seq_len):
            idx = jnp.arange(seq_len, dtype=jnp.float32)
            d = jnp.abs(idx[None, :] - idx[:, None])
            return jnp.clip(d, 0.0, MAX_DISTANCE) * SCALE
        B, S, _ = x.shape
        f = x @ W + b
        e = jnp.einsum('bsd,btd->bst', f, f)
        e = e + distance_bias(S)[None, :, :]
        a = jax.nn.softmax(e, axis=-1)
        out = jnp.einsum('bst,btd->bsd', a, f)
        return out

    def _L0_ffn_ref(x, W_r, W_k, W_v, mu_r, mu_k):
        import jax, jax.numpy as jnp
        import numpy as np
        DIM = 128

        def _reference_tuple_inner(x, W_r, W_k, W_v, mu_r, mu_k):
            B, T, C = x.shape
            x_prev = jnp.concatenate([jnp.zeros((B, 1, C), x.dtype), x[:, :-1, :]], axis=1)
            xr = mu_r * x + (1.0 - mu_r) * x_prev
            xk = mu_k * x + (1.0 - mu_k) * x_prev
            r = jax.nn.sigmoid(jnp.einsum('btc,dc->btd', xr, W_r))
            k = jnp.einsum('btc,dc->btd', xk, W_k)
            k_act = jnp.square(jax.nn.relu(k))
            out = r * jnp.einsum('btc,dc->btd', k_act, W_v)
            new_state = x[:, -1, :]
            return (out, new_state)
        return _reference_tuple_inner(x, W_r, W_k, W_v, mu_r, mu_k)[0]
    x = L0_attn_x
    mod = (_silu(L0_c) @ L0_wmod).reshape(L0_c.shape[0], 6, 1, -1)
    sa, ca, ga, sb, cb, gb = (mod[:, 0], mod[:, 1], mod[:, 2], mod[:, 3], mod[:, 4], mod[:, 5])
    ga = (2 * (ga >= 0) - 1) * jnp.maximum(jnp.abs(ga), 0.25)
    gb = (2 * (gb >= 0) - 1) * jnp.maximum(jnp.abs(gb), 0.25)
    h = _layernorm(x, axis=-1) * (1 + ca) + sa
    x = x + ga * _L0_attn_ref(h, L0_attn_W, L0_attn_b)
    h = _layernorm(x, axis=-1) * (1 + cb) + sb
    x = x + gb * _L0_ffn_ref(h, L0_ffn_W_r, L0_ffn_W_k, L0_ffn_W_v, L0_ffn_mu_r, L0_ffn_mu_k)
    return x

_drawn_inputs = setup_inputs


def setup_inputs(seed=0):
    import zlib

    import numpy as np

    out = dict(_drawn_inputs(seed))
    spreads = {'L0_attn_b': (0.0, 0.308)}
    factors = {'L0_ffn_W_r': 8.0,
     'L0_ffn_W_k': 3.071,
     'L0_ffn_W_v': 2.839,
     'L0_ffn_mu_r': 8.0,
     'L0_ffn_mu_k': 4.788}
    for name, (base, spread) in spreads.items():
        noise = np.random.default_rng([zlib.crc32(name.encode()), seed]).standard_normal(out[name].shape)
        drawn = base * np.exp(spread * noise) if base else spread * noise
        out[name] = jnp.asarray(drawn.astype(out[name].dtype))
    for name, factor in factors.items():
        out[name] = (out[name] * factor).astype(out[name].dtype)
    return out
```

```python
from contextlib import ExitStack

import concourse.bass as bass
from concourse import mybir

ALU = mybir.AluOpType
ACT = mybir.ActivationFunctionType
F32 = mybir.dt.float32
F32R = mybir.dt.float32r
I32 = mybir.dt.int32

P = 128
EPS = 1e-5
MAX_DISTANCE = 10
SCALE = 0.01
GATE_MIN = 0.25
LOWEST = -3.0e38


def adaln_attention_channelmix_kernel(
    nc: bass.Bass,
    x: bass.AP,
    attn_w: bass.AP,
    attn_b: bass.AP,
    w_r: bass.AP,
    w_k: bass.AP,
    w_v: bass.AP,
    mu_r: bass.AP,
    mu_k: bass.AP,
    cond: bass.AP,
    wmod: bass.AP,
    out: bass.AP,
):
    B, S, D = x.shape
    NT = S // P
    WIDE = (2 * NT - 1) * P
    assert D == P and S == NT * P and NT == 4

    with ExitStack() as ctx:
        def sb(name, shape, dt=F32):
            return ctx.enter_context(nc.sbuf_tensor(name, shape, dt))

        def bank(name):
            return ctx.enter_context(nc.psum_tensor(name, [P, 512], F32))

        def sem(name):
            return ctx.enter_context(nc.semaphore(name))

        ident = sb("ident", [P, P])
        ident_r = sb("ident_r", [P, P], F32R)
        ones_r = sb("ones_r", [2, P], F32R)
        offs = sb("offs", [P, WIDE], I32)
        dist = sb("dist", [P, WIDE])
        absd = sb("absd", [P, WIDE])
        bias = sb("bias", [P, WIDE])
        neg_half = sb("neg_half", [P, NT])
        wa = sb("wa", [P, D])
        ffn_w = sb("ffn_w", [P, 3, D])
        ffn_wT = sb("ffn_wT", [P, 3, D])
        wrT, wkT, wvT = (ffn_wT[:, n] for n in range(3))
        vecs = sb("vecs", [P, 3])
        c_sb = sb("c_sb", [B, D])
        wm = sb("wm", [P, 6 * D])
        th_c = sb("th_c", [P, B])
        cT = sb("cT", [P, B])
        silu2 = sb("silu2", [P, B])
        silu = sb("silu", [P, B])
        modT = sb("modT", [P, 4, B])
        gate_raw = sb("gate_raw", [B, 2, D])
        gate_two = sb("gate_two", [B, 2, D])
        gate_sign = sb("gate_sign", [B, 2, D])
        gate_abs = sb("gate_abs", [B, 2, D])
        gate = sb("gate", [B, 2, D])
        gates = sb("gates", [P, B, 2, D])
        xs = sb("xs", [P, B, NT, D])
        ys = sb("ys", [P, B, NT, D])
        st1 = sb("st1", [P, NT, 6])
        mv1 = sb("mv1", [P, NT, 2])
        ve1 = sb("ve1", [P, NT])
        nm1 = sb("nm1", [P, NT])
        rstd1 = sb("rstd1", [P, NT])
        sh1 = sb("sh1", [P, NT])
        xn = sb("xn", [P, NT, D])
        hT = sb("hT", [P, S])
        fT = sb("fT", [P, S])
        fT_hi = sb("fT_hi", [P, S], F32R)
        fT_lo = sb("fT_lo", [P, S], F32R)
        ftok = sb("ftok", [P, NT, D + 1])
        mx = sb("mx", [P, NT])
        nmx = sb("nmx", [P, NT, 2], F32R)
        nmx_row = sb("nmx_row", [2, S], F32R)
        pT = sb("pT", [P, NT, S])
        rl = sb("rl", [P, NT])
        st2 = sb("st2", [P, NT, 6])
        mv2 = sb("mv2", [P, NT, 2])
        ve2 = sb("ve2", [P, NT])
        nm2 = sb("nm2", [P, NT])
        rstd2 = sb("rstd2", [P, NT])
        sh2 = sb("sh2", [P, NT])
        xn2 = sb("xn2", [P, NT, D])
        h2T = sb("h2T", [P, S + 1])
        dT = sb("dT", [P, S])
        xkT = sb("xkT", [P, S])
        xrT = sb("xrT", [P, S])
        krT = sb("krT", [P, S])
        kaT = sb("kaT", [P, S])
        wv_g = sb("wv_g", [P, D])
        th_r = sb("th_r", [P, S])
        gv = sb("gv", [P, S])

        gate_dram = nc.dram_tensor("gate_dram", (B, 2 * D), F32).ap()

        E = [bank(f"scores{i}") for i in range(NT)]
        O = [bank(f"pv{i}") for i in range(2)]
        A = bank("bank_a")
        C = bank("bank_c")

        x_in = [sem(f"x_in{b}") for b in range(3)]
        x_rest = sem("x_rest")
        c_in = sem("c_in")
        wmod_in = sem("wmod_in")
        wa_in = sem("wa_in")
        w_in = sem("w_in")
        pool_const = sem("pool_const")
        consts = sem("consts")
        setup_pe = sem("setup_pe")
        setup_act = sem("setup_act")
        setup_dve = sem("setup_dve")
        gates_out = sem("gates_out")
        gates_in = sem("gates_in")
        dve_st1, dve_mv1, pool_ve1, pool_rstd1, pool_sh1 = (
            sem(n) for n in ("dve_st1", "dve_mv1", "pool_ve1", "pool_rstd1", "pool_sh1"))
        act_xn, pe_xnT, act_hT, pe_fT, act_fT, act_fT_hi, dve_fT_lo = (
            sem(n) for n in ("act_xn", "pe_xnT", "act_hT", "pe_fT", "act_fT", "act_fT_hi", "dve_fT_lo"))
        pe_ftok, dve_ftok, pe_scores, dve_max, dve_nmx_hi, dve_nmx, pe_nmx, act_nmx = (
            sem(n) for n in ("pe_ftok", "dve_ftok", "pe_scores", "dve_max", "dve_nmx_hi", "dve_nmx",
                             "pe_nmx", "act_nmx"))
        pe_shift, act_exp, pe_pv, dve_rl, dve_x1 = (
            sem(n) for n in ("pe_shift", "act_exp", "pe_pv", "dve_rl", "dve_x1"))
        dve_st2, dve_mv2, pool_ve2, pool_rstd2, pool_sh2 = (
            sem(n) for n in ("dve_st2", "dve_mv2", "pool_ve2", "pool_rstd2", "pool_sh2"))
        act_xn2, pe_h2T, act_h2T, pool_d, dve_xk, dve_xr = (
            sem(n) for n in ("act_xn2", "pe_h2T", "act_h2T", "pool_d", "dve_xk", "dve_xr"))
        pe_k, act_relu, pool_ka, pool_wv, pe_r, act_tanh, pe_v, dve_gv, pool_y, stored = (
            sem(n) for n in ("pe_k", "act_relu", "pool_ka", "pool_wv", "pe_r", "act_tanh", "pe_v",
                             "dve_gv", "pool_y", "stored"))

        def blk(j):
            return slice(j * P, (j + 1) * P)

        def at_least(eng, s, value):
            if value > 0:
                eng.wait_ge(s, value)

        def has(b):
            return 0 <= b < B

        STEPS = range(-2, B + 2)

        block = ctx.enter_context(nc.Block())

        @block.sync
        def _(sp):
            def load_x(b, s):
                sp.dma_start(xs[:, b], x[b].rearrange("(j p) d -> p j d", p=P)).then_inc(s, 16)

            load_x(0, x_in[0])
            sp.dma_start(wa[:], attn_w).then_inc(wa_in, 16)
            for n, v in enumerate((attn_b, mu_r, mu_k)):
                sp.dma_start(vecs[:, n:n + 1], v.rearrange("(p a) -> p a", a=1)).then_inc(wa_in, 16)
            load_x(1, x_in[1])
            load_x(2, x_in[2])
            for n, dram in enumerate((w_r, w_k, w_v)):
                sp.dma_start(ffn_w[:, n], dram).then_inc(w_in, 16)
            sp.wait_ge(setup_dve, 6)
            sp.dma_start(gate_dram, gate[:].rearrange("b g d -> b (g d)")).then_inc(gates_out, 16)
            sp.wait_ge(gates_out, 16)
            sp.dma_start(gates[:].rearrange("p b g d -> p (b g d)"),
                         gate_dram.rearrange("(a b) n -> a (b n)", a=1).to_broadcast([P, 2 * B * D])).then_inc(gates_in, 16)
            for b in range(3, B):
                load_x(b, x_rest)
            for b in range(B):
                sp.wait_ge(pool_y, b + 1)
                sp.dma_start(out[b].rearrange("(j p) d -> p j d", p=P), ys[:, b]).then_inc(stored, 16)
            sp.wait_ge(stored, 16 * B)

        @block.gpsimd
        def _(pool):
            pool.memset(ident[:], 0.0).then_inc(pool_const, 1)
            pool.memset(neg_half[:], -0.5).then_inc(pool_const, 1)
            pool.wait_ge(pool_const, 2)
            pool.affine_select(out=ident[:], in_=ident[:], compare_op=ALU.not_equal, fill=1.0,
                               base=0, pattern=[[-1, P]], channel_multiplier=1).then_inc(pool_const, 1)
            pool.iota(offs[:], pattern=[[1, WIDE]], base=-(NT - 1) * P, channel_multiplier=-1).then_inc(pool_const, 1)

            def rstd(b, mv, ve, nm, rs, sh, s_mv, s_ve, s_rstd, s_sh):
                pool.wait_ge(s_mv, b + 1)
                pool.tensor_scalar(ve[:], mv[:, :, 1], EPS, 1.0, ALU.add, ALU.mult).then_inc(s_ve, 1)
                pool.tensor_scalar(nm[:], mv[:, :, 0], -1.0, 0.0, ALU.mult, ALU.add).then_inc(s_ve, 1)
                pool.wait_ge(s_ve, 2 * b + 2)
                pool.tensor_tensor(rs[:], ve[:], neg_half[:], ALU.pow).then_inc(s_rstd, 1)
                pool.wait_ge(s_rstd, b + 1)
                pool.tensor_tensor(sh[:], nm[:], rs[:], ALU.mult).then_inc(s_sh, 1)

            for t in STEPS:
                if has(t - 1):
                    b = t - 1
                    at_least(pool, act_xn2, b)
                    rstd(b, mv2, ve2, nm2, rstd2, sh2, dve_mv2, pool_ve2, pool_rstd2, pool_sh2)
                    if b == 0:
                        pool.wait_ge(gates_in, 16)
                        pool.wait_ge(setup_act, 3)
                    at_least(pool, pe_v, b)
                    pool.tensor_tensor(wv_g[:], wvT, gates[:, b, 1], ALU.mult).then_inc(pool_wv, 1)
                    pool.wait_ge(act_h2T, b + 1)
                    at_least(pool, dve_xr, b)
                    pool.tensor_tensor(dT[:], h2T[:, 1:S + 1], h2T[:, 0:S], ALU.subtract).then_inc(pool_d, 1)
                if has(t - 2):
                    b = t - 2
                    pool.wait_ge(dve_gv, b + 1)
                    pool.tensor_tensor(ys[:, b], xs[:, b], gv[:].rearrange("p (j d) -> p j d", j=NT),
                                       ALU.add).then_inc(pool_y, 1)
                if has(t + 2):
                    b = t + 2
                    at_least(pool, act_xn, b)
                    rstd(b, mv1, ve1, nm1, rstd1, sh1, dve_mv1, pool_ve1, pool_rstd1, pool_sh1)
                if has(t - 1):
                    b = t - 1
                    pool.wait_ge(act_relu, b + 1)
                    at_least(pool, pe_v, b)
                    pool.tensor_tensor(kaT[:], krT[:], krT[:], ALU.mult).then_inc(pool_ka, 1)

        @block.scalar
        def _(act):
            act.dma_start(c_sb[:], cond).then_inc(c_in, 16)
            act.dma_start(wm[:], wmod).then_inc(wmod_in, 16)
            act.wait_ge(setup_pe, 1)
            act.activation(th_c[:], A[:, 0:B], ACT.Tanh, scale=0.5).then_inc(setup_act, 1)
            act.copy(cT[:], A[:, 0:B]).then_inc(setup_act, 1)

            def weights():
                act.wait_ge(setup_pe, 4)
                act.copy(ffn_wT[:], C[:, 0:3 * P].rearrange("p (n d) -> p n d", n=3)).then_inc(setup_act, 1)

            for t in STEPS:
                if t == -1:
                    weights()
                if has(t - 1):
                    b = t - 1
                    act.wait_ge(pool_sh2, b + 1)
                    at_least(act, pe_h2T, b)
                    for j in range(NT):
                        ins = act.activation(xn2[:, j], xs[:, b, j], ACT.Identity,
                                             scale=rstd2[:, j:j + 1], bias=sh2[:, j:j + 1])
                    ins.then_inc(act_xn2, 1)
                    act.wait_ge(pe_h2T, b + 1)
                    at_least(act, dve_xr, b)
                    act.activation(h2T[:, 1:S + 1], C[:], ACT.Identity, scale=modT[:, 3, b:b + 1],
                                   bias=modT[:, 2, b:b + 1]).then_inc(act_h2T, 1)
                if has(t):
                    act.wait_ge(pe_nmx, t + 1)
                    at_least(act, pe_shift, NT * t)
                    act.copy(nmx_row[:], O[0][0:2, :]).then_inc(act_nmx, 1)
                if has(t + 1):
                    b = t + 1
                    act.wait_ge(pe_xnT, b + 1)
                    at_least(act, pe_fT, b)
                    if b == 0:
                        act.wait_ge(setup_dve, 7)
                    act.activation(hT[:], O[1][:], ACT.Identity, scale=modT[:, 1, b:b + 1],
                                   bias=modT[:, 0, b:b + 1]).then_inc(act_hT, 1)
                if has(t):
                    for i in range(NT):
                        act.wait_ge(pe_shift, NT * t + i + 1)
                        if i == 0:
                            at_least(act, pe_pv, 2 * t)
                        act.activation(pT[:, i], E[i][:], ACT.Exp).then_inc(act_exp, 1)
                if has(t + 1):
                    b = t + 1
                    act.wait_ge(pe_fT, b + 1)
                    if b == 0:
                        act.wait_ge(wa_in, 64)
                    at_least(act, pe_ftok, b)
                    at_least(act, dve_fT_lo, b)
                    act.activation(fT[:], C[:], ACT.Identity, bias=vecs[:, 0:1]).then_inc(act_fT, 1)
                    act.activation(fT_hi[:], C[:], ACT.Identity, bias=vecs[:, 0:1]).then_inc(act_fT_hi, 1)
                if has(t - 1):
                    b = t - 1
                    act.wait_ge(pe_k, b + 1)
                    at_least(act, pool_ka, b)
                    act.activation(krT[:], A[:], ACT.Relu).then_inc(act_relu, 1)
                if has(t + 2):
                    b = t + 2
                    act.wait_ge(pool_sh1, b + 1)
                    at_least(act, pe_xnT, b)
                    for j in range(NT):
                        ins = act.activation(xn[:, j], xs[:, b, j], ACT.Identity,
                                             scale=rstd1[:, j:j + 1], bias=sh1[:, j:j + 1])
                    ins.then_inc(act_xn, 1)
                if has(t - 1):
                    b = t - 1
                    act.wait_ge(pe_r, b + 1)
                    at_least(act, dve_gv, b)
                    act.activation(th_r[:], C[:], ACT.Tanh, scale=0.5).then_inc(act_tanh, 1)

        @block.vector
        def _(dve):
            dve.memset(h2T[:, 0:1], 0.0).then_inc(consts, 1)
            dve.memset(ones_r[:].bitcast(F32), 1.0).then_inc(consts, 1)
            dve.memset(ftok[:, :, D:D + 1], 1.0).then_inc(consts, 1)
            dve.wait_ge(pool_const, 4)
            dve.tensor_copy(ident_r[:], ident[:]).then_inc(consts, 1)

            def stats(b, st, mv, s_st, s_mv):
                for j in range(NT):
                    dve.bn_stats(st[:, j], xs[:, b, j]).then_inc(s_st, 1)
                for j in range(NT):
                    dve.wait_ge(s_st, NT * b + j + 1)
                    ins = dve.bn_aggr(mv[:, j], st[:, j])
                ins.then_inc(s_mv, 1)

            def stats1(b):
                if b < 3:
                    dve.wait_ge(x_in[b], 16)
                if b == 3:
                    dve.wait_ge(x_rest, 16 * (B - 3))
                at_least(dve, pool_ve1, 2 * b)
                at_least(dve, dve_mv1, b)
                stats(b, st1, mv1, dve_st1, dve_mv1)

            stats1(0)
            dve.wait_ge(setup_act, 2)
            dve.scalar_tensor_tensor(silu2[:], th_c[:], 1.0, cT[:], ALU.add, ALU.mult).then_inc(setup_dve, 1)
            dve.wait_ge(setup_dve, 1)
            dve.tensor_scalar(silu[:], silu2[:], 0.5, None, ALU.mult).then_inc(setup_dve, 1)
            dve.wait_ge(setup_pe, 2)
            dve.tensor_copy(gate_raw[:], O[0][0:B, 0:2 * D].rearrange("b (g d) -> b g d", g=2)).then_inc(setup_dve, 1)
            dve.wait_ge(setup_dve, 3)
            dve.tensor_scalar(gate_two[:], gate_raw[:], 0.0, 2.0, ALU.is_ge, ALU.mult).then_inc(setup_dve, 1)
            dve.wait_ge(setup_dve, 4)
            dve.tensor_scalar(gate_sign[:], gate_two[:], -1.0, None, ALU.add).then_inc(setup_dve, 1)
            dve.wait_ge(setup_dve, 5)
            dve.tensor_tensor(gate_abs[:], gate_raw[:], gate_sign[:], ALU.mult).then_inc(consts, 1)
            dve.wait_ge(consts, 5)
            dve.scalar_tensor_tensor(gate[:, 0], gate_abs[:, 0], GATE_MIN, gate_sign[:, 0], ALU.max, ALU.mult).then_inc(consts, 1)
            dve.tensor_scalar(gate_raw[:, 1], gate_abs[:, 1], GATE_MIN, 0.5, ALU.max, ALU.mult).then_inc(consts, 1)
            dve.wait_ge(consts, 7)
            dve.tensor_tensor(gate[:, 1], gate_raw[:, 1], gate_sign[:, 1], ALU.mult).then_inc(setup_dve, 1)
            dve.wait_ge(setup_pe, 3)
            md = O[1][:, 0:4 * B].rearrange("p (m b) -> p m b", m=4)
            dve.tensor_copy(modT[:, 0:4:2], md[:, 0:4:2]).then_inc(consts, 1)
            dve.tensor_scalar(modT[:, 1:4:2], md[:, 1:4:2], 1.0, None, ALU.add).then_inc(setup_dve, 1)
            dve.wait_ge(consts, 8)
            stats1(1)
            dve.tensor_copy(dist[:], offs[:]).then_inc(consts, 1)
            dve.wait_ge(consts, 9)
            dve.scalar_tensor_tensor(absd[:], dist[:], -1.0, dist[:], ALU.mult, ALU.max).then_inc(consts, 1)
            dve.wait_ge(consts, 10)
            dve.tensor_scalar(bias[:], absd[:], float(MAX_DISTANCE), SCALE, ALU.min, ALU.mult).then_inc(consts, 1)

            for t in STEPS:
                if has(t):
                    for i in range(NT):
                        dve.wait_ge(pe_scores, NT * t + i + 1)
                        if t == 0 and i == 0:
                            dve.wait_ge(consts, 11)
                        if i == 0:
                            at_least(dve, dve_nmx, t)
                        dve.tensor_tensor_reduce(E[i][:], E[i][:], bias[:, (NT - 1 - i) * P:(NT - 1 - i) * P + S],
                                                 1.0, LOWEST, ALU.add, ALU.max, mx[:, i:i + 1]).then_inc(dve_max, 1)
                    dve.wait_ge(dve_max, NT * (t + 1))
                    at_least(dve, pe_nmx, t)
                    dve.tensor_scalar(nmx[:, :, 0], mx[:], -1.0, None, ALU.mult).then_inc(dve_nmx_hi, 1)
                    dve.wait_ge(dve_nmx_hi, t + 1)
                    dve.scalar_tensor_tensor(nmx[:, :, 1], mx[:], -1.0, nmx[:, :, 0].bitcast(F32), ALU.mult,
                                             ALU.subtract).then_inc(dve_nmx, 1)
                    dve.wait_ge(pe_ftok, t + 1)
                    at_least(dve, pe_pv, 2 * t)
                    if t == 0:
                        dve.wait_ge(gates_in, 16)
                    dve.tensor_tensor(ftok[:, :, 0:D], A[:].rearrange("p (j d) -> p j d", j=NT),
                                      gates[:, t, 0:1].to_broadcast([P, NT, D]), ALU.mult).then_inc(dve_ftok, 1)
                if has(t + 2) and t + 2 >= 2:
                    stats1(t + 2)
                if has(t - 1):
                    b = t - 1
                    dve.wait_ge(pool_d, b + 1)
                    at_least(dve, pe_k, b)
                    dve.scalar_tensor_tensor(xkT[:], dT[:], vecs[:, 2:3], h2T[:, 0:S], ALU.mult, ALU.add).then_inc(dve_xk, 1)
                    at_least(dve, pe_r, b)
                    dve.scalar_tensor_tensor(xrT[:], dT[:], vecs[:, 1:2], h2T[:, 0:S], ALU.mult, ALU.add).then_inc(dve_xr, 1)
                if has(t + 1):
                    b = t + 1
                    dve.wait_ge(act_fT_hi, b + 1)
                    at_least(dve, pe_scores, NT * b)
                    dve.tensor_tensor(fT_lo[:], fT[:], fT_hi[:].bitcast(F32), ALU.subtract).then_inc(dve_fT_lo, 1)
                if has(t):
                    for h in range(2):
                        ob = O[h][:, 0:2 * (D + 1)].rearrange("p (j d) -> p j d", j=2)
                        dve.wait_ge(pe_pv, 2 * t + h + 1)
                        if h == 0:
                            at_least(dve, dve_x1, NT * t)
                        dve.reciprocal(rl[:, 2 * h:2 * h + 2], ob[:, :, D]).then_inc(dve_rl, 1)
                        dve.wait_ge(dve_rl, 2 * t + h + 1)
                        for j in range(2):
                            n = 2 * h + j
                            dve.scalar_tensor_tensor(xs[:, t, n], ob[:, j, 0:D], rl[:, n:n + 1], xs[:, t, n],
                                                     ALU.mult, ALU.add).then_inc(dve_x1, 1)
                    at_least(dve, pool_ve2, 2 * t)
                    at_least(dve, dve_mv2, t)
                    for j in range(NT):
                        dve.wait_ge(dve_x1, NT * t + j + 1)
                        dve.bn_stats(st2[:, j], xs[:, t, j]).then_inc(dve_st2, 1)
                    for j in range(NT):
                        dve.wait_ge(dve_st2, NT * t + j + 1)
                        ins = dve.bn_aggr(mv2[:, j], st2[:, j])
                    ins.then_inc(dve_mv2, 1)
                if has(t - 1):
                    b = t - 1
                    dve.wait_ge(pe_v, b + 1)
                    dve.wait_ge(act_tanh, b + 1)
                    at_least(dve, pool_y, b)
                    dve.scalar_tensor_tensor(gv[:], th_r[:], 1.0, A[:], ALU.add, ALU.mult).then_inc(dve_gv, 1)

        @block.tensor
        def _(pe):
            pe.wait_ge(c_in, 16)
            pe.wait_ge(pool_const, 3)
            pe.transpose(A[:, 0:B], c_sb[:], ident[0:B, 0:B]).then_inc(setup_pe, 1)
            pe.wait_ge(setup_dve, 2)
            pe.wait_ge(wmod_in, 16)
            wm6 = wm[:].rearrange("p (m d) -> p m d", m=6)
            pe.matmul(O[0][0:B, 0:2 * D].rearrange("b (g d) -> b g d", g=2), silu[:], wm6[:, 2:6:3],
                      start=True, stop=True).then_inc(setup_pe, 1)
            for n, m in enumerate((0, 1, 3, 4)):
                mm = pe.matmul(O[1][:, n * B:(n + 1) * B], wm6[:, m], silu[:], start=True, stop=True)
            mm.then_inc(setup_pe, 1)

            pe.wait_ge(w_in, 48)
            for n in range(3):
                mm = pe.transpose(C[:, blk(n)], ffn_w[:, n], ident[:])
            mm.then_inc(setup_pe, 1)

            for t in STEPS:
                if has(t):
                    pe.wait_ge(dve_fT_lo, t + 1)
                    for i in range(NT):
                        at_least(pe, act_exp, NT * (t - 1) + i + 1)
                        pe.matmul(E[i][:], fT_lo[:, blk(i)], fT_hi[:], start=True, stop=False)
                        pe.matmul(E[i][:], fT_hi[:, blk(i)], fT_lo[:], start=False, stop=False)
                        pe.matmul(E[i][:], fT_hi[:, blk(i)], fT_hi[:], start=False, stop=True).then_inc(pe_scores, 1)
                    at_least(pe, dve_gv, t - 1)
                    for j in range(NT):
                        mm = pe.transpose(A[:, blk(j)], fT[:, blk(j)], ident[:])
                    mm.then_inc(pe_ftok, 1)
                if has(t - 1):
                    b = t - 1
                    pe.wait_ge(act_xn2, b + 1)
                    at_least(pe, act_tanh, b)
                    for j in range(NT):
                        mm = pe.transpose(C[:, blk(j)], xn2[:, j], ident[:])
                    mm.then_inc(pe_h2T, 1)
                if has(t + 1):
                    b = t + 1
                    pe.wait_ge(act_xn, b + 1)
                    if b == 0:
                        pe.wait_ge(setup_dve, 7)
                    at_least(pe, dve_x1, NT * (b - 1))
                    for j in range(NT):
                        mm = pe.transpose(O[1][:, blk(j)], xn[:, j], ident[:])
                    mm.then_inc(pe_xnT, 1)
                if has(t):
                    pe.wait_ge(dve_nmx, t + 1)
                    if t == 0:
                        pe.wait_ge(setup_dve, 3)
                    at_least(pe, dve_x1, NT * t)
                    for j in range(NT):
                        mm = pe.transpose(O[0][0:2, blk(j)].bitcast(F32R), nmx[:, j], ident_r[:])
                    mm.then_inc(pe_nmx, 1)
                    pe.wait_ge(act_nmx, t + 1)
                    for i in range(NT):
                        pe.matmul(E[i][:], ones_r[:], nmx_row[:], start=False, stop=True,
                                  skip_group_check=True).then_inc(pe_shift, 1)
                if has(t + 1):
                    b = t + 1
                    pe.wait_ge(act_hT, b + 1)
                    at_least(pe, act_h2T, t)
                    if b == 0:
                        pe.wait_ge(wa_in, 64)
                        pe.wait_ge(setup_act, 3)
                    pe.matmul(C[:], wa[:], hT[:], start=True, stop=True).then_inc(pe_fT, 1)

                def pv(k):
                    pe.wait_ge(act_exp, NT * t + k + 1)
                    for n in range(NT):
                        h, j = divmod(n, 2)
                        mm = pe.matmul(O[h][:, j * (D + 1):(j + 1) * (D + 1)], pT[:, k, blk(n)], ftok[:, k],
                                       start=(k == 0 and j == 0), stop=(k == NT - 1), skip_group_check=True)
                        if k == NT - 1 and j == 1:
                            mm.then_inc(pe_pv, 1)

                if has(t):
                    pe.wait_ge(dve_ftok, t + 1)
                    pv(0)
                    pv(1)
                if has(t - 1):
                    b = t - 1
                    pe.wait_ge(dve_xk, b + 1)
                    pe.matmul(A[:], wkT, xkT[:], start=True, stop=True).then_inc(pe_k, 1)
                if has(t):
                    pv(2)
                    pv(3)
                if has(t - 1):
                    b = t - 1
                    pe.wait_ge(dve_xr, b + 1)
                    if has(t + 1):
                        pe.wait_ge(act_fT_hi, t + 2)
                    for j in range(NT):
                        mm = pe.matmul(C[:, blk(j)], xrT[:, blk(j)], wrT, start=True, stop=True)
                    mm.then_inc(pe_r, 1)
                    pe.wait_ge(pool_ka, b + 1)
                    for j in range(NT):
                        mm = pe.matmul(A[:, blk(j)], kaT[:, blk(j)], wv_g[:], start=True, stop=True)
                    mm.then_inc(pe_v, 1)


_INS = ["L0_attn_x", "L0_attn_W", "L0_attn_b", "L0_ffn_W_r", "L0_ffn_W_k", "L0_ffn_W_v", "L0_ffn_mu_r",
        "L0_ffn_mu_k", "L0_c", "L0_wmod"]
_OUTS = [((8, 512, 128), "float32")]


def kernel(**inputs):
    import numpy as _np
    import concourse.bacc as _bacc
    from concourse import mybir as _mybir
    from concourse.bass_utils import run_bass_kernel_spmd as _run

    nc = _bacc.Bacc("TRN2", target_bir_lowering=False, num_devices=1)
    arrays, args = {}, []
    for name in _INS:
        a = _np.ascontiguousarray(inputs[name])
        arrays[f"in_{name}_dram"] = a
        args.append(nc.dram_tensor(f"in_{name}_dram", a.shape, _mybir.dt.from_np(a.dtype), kind="ExternalInput").ap())
    for i, (shape, dtype) in enumerate(_OUTS):
        dt = _mybir.dt.from_np(_np.dtype(dtype))
        args.append(nc.dram_tensor(f"out_{i}_dram", shape, dt, kind="ExternalOutput").ap())
    adaln_attention_channelmix_kernel(nc, *args)
    r = _run(nc, [arrays], core_ids=[0])
    return r.results[0]["out_0_dram"]
```

```python
from contextlib import ExitStack

import concourse.bass as bass
from concourse import mybir

ALU = mybir.AluOpType
ACT = mybir.ActivationFunctionType
F32 = mybir.dt.float32
F32R = mybir.dt.float32r
I32 = mybir.dt.int32

P = 128
EPS = 1e-5
MAX_DISTANCE = 10
SCALE = 0.01
GATE_MIN = 0.25
LOWEST = -3.0e38
WARM = (5, 4, 4)


def adaln_attention_channelmix_kernel(
    nc: bass.Bass,
    x: bass.AP,
    attn_w: bass.AP,
    attn_b: bass.AP,
    w_r: bass.AP,
    w_k: bass.AP,
    w_v: bass.AP,
    mu_r: bass.AP,
    mu_k: bass.AP,
    cond: bass.AP,
    wmod: bass.AP,
    out: bass.AP,
):
    B, S, D = x.shape
    NT = S // P
    H = S // 2
    WIDE = (2 * NT - 1) * P
    assert D == P and S == NT * P and NT == 4

    with ExitStack() as ctx:
        def sb(name, shape, dt=F32):
            return ctx.enter_context(nc.sbuf_tensor(name, shape, dt))

        def bank(name):
            return ctx.enter_context(nc.psum_tensor(name, [P, 512], F32))

        def sem(name):
            return ctx.enter_context(nc.semaphore(name))

        ident = sb("ident", [P, P])
        ident_r = sb("ident_r", [P, P], F32R)
        ones_r = sb("ones_r", [2, P], F32R)
        offs = sb("offs", [P, WIDE], I32)
        absd = sb("absd", [P, WIDE])
        bias = sb("bias", [P, WIDE])
        neg_half = sb("neg_half", [P, NT])
        wa = sb("wa", [P, D])
        ffn_w = sb("ffn_w", [P, 3, D])
        ffn_wT = sb("ffn_wT", [P, 3, D])
        wrT, wkT, wvT = (ffn_wT[:, n] for n in range(3))
        vecs = sb("vecs", [P, 3])
        b_col, mu_r_col, mu_k_col = (vecs[:, n:n + 1] for n in range(3))
        c_sb = sb("c_sb", [B, D])
        wm = sb("wm", [P, 6 * D])
        th_c = sb("th_c", [P, B])
        cT = sb("cT", [P, B])
        silu2 = sb("silu2", [P, B])
        silu = sb("silu", [P, B])
        modT = sb("modT", [P, B, 4])
        gate_raw = sb("gate_raw", [B, 2, D])
        gate_two = sb("gate_two", [B, 2, D])
        gate_sign = sb("gate_sign", [B, 2, D])
        gate_abs = sb("gate_abs", [B, 2, D])
        gate_half = sb("gate_half", [B, D])
        gate = sb("gate", [B, 2, D])
        gates = sb("gates", [P, B, 2, D])
        gate_dram = nc.dram_tensor("gate_dram", (B, 2 * D), F32).ap()
        xs = sb("xs", [P, B, NT, D])
        ys = sb("ys", [P, B, NT, D])
        st1, mv1, ve1, nm1, rstd1, sh1 = (
            sb(n, [P, NT] + d) for n, d in (("st1", [6]), ("mv1", [2]), ("ve1", []), ("nm1", []),
                                            ("rstd1", []), ("sh1", [])))
        st2, mv2, ve2, nm2, rstd2, sh2 = (
            sb(n, [P, NT] + d) for n, d in (("st2", [6]), ("mv2", [2]), ("ve2", []), ("nm2", []),
                                            ("rstd2", []), ("sh2", [])))
        xn = sb("xn", [P, NT, D])
        hT = sb("hT", [P, S])
        fT = sb("fT", [P, S])
        fT_hi = sb("fT_hi", [P, S], F32R)
        fT_lo = sb("fT_lo", [P, S], F32R)
        ftok = sb("ftok", [P, NT, D + 1])
        mx = sb("mx", [P, NT])
        nmx = sb("nmx", [P, NT, 2], F32R)
        nmx_row = sb("nmx_row", [2, S], F32R)
        pT = sb("pT", [P, NT, S])
        rl = sb("rl", [P, NT])
        xn2 = sb("xn2", [P, NT, D])
        h2T = sb("h2T", [P, S + 1])
        dT = sb("dT", [P, S])
        xkT = sb("xkT", [P, S])
        xrT = sb("xrT", [P, S])
        krT = sb("krT", [P, S])
        kaT = sb("kaT", [P, S])
        wv_g = sb("wv_g", [P, D])
        th_r = sb("th_r", [P, S])
        gv = sb("gv", [P, S])

        E = [bank(f"scores{i}") for i in range(NT)]
        O = [bank(f"pv{i}") for i in range(2)]
        A = bank("bank_a")
        C = bank("bank_c")

        x0_in = [sem(f"x0_in{h}") for h in range(2)]
        x1_in, x2_in, x_rest_in, c_in, wmod_in, wa_in, w_in = (
            sem(n) for n in ("x1_in", "x2_in", "x_rest_in", "c_in", "wmod_in", "wa_in", "w_in"))
        pool_ident, pool_offs, act_absd, dve_const, dve_bias = (
            sem(n) for n in ("pool_ident", "pool_offs", "act_absd", "dve_const", "dve_bias"))
        pe_cT, act_cT, dve_silu, pe_mod, dve_mod, pe_gate, dve_gate, gate_out, gates_in, pe_wT, act_wT = (
            sem(n) for n in ("pe_cT", "act_cT", "dve_silu", "pe_mod", "dve_mod", "pe_gate", "dve_gate",
                             "gate_out", "gates_in", "pe_wT", "act_wT"))
        dve_st1, dve_mv1, pool_ve1, pool_rstd1, pool_sh1 = (
            sem(n) for n in ("dve_st1", "dve_mv1", "pool_ve1", "pool_rstd1", "pool_sh1"))
        act_xn, pe_xnT, act_hT, pe_fT, act_fT, act_fT_hi, pool_fT_lo, dve_fT_lo0 = (
            sem(n) for n in ("act_xn", "pe_xnT", "act_hT", "pe_fT", "act_fT", "act_fT_hi", "pool_fT_lo",
                             "dve_fT_lo0"))
        pe_ftok, dve_ftok, pe_scores, dve_max, dve_nmx_hi, dve_nmx, pe_nmx, act_nmx = (
            sem(n) for n in ("pe_ftok", "dve_ftok", "pe_scores", "dve_max", "dve_nmx_hi", "dve_nmx",
                             "pe_nmx", "act_nmx"))
        pe_shift, act_exp, pe_pv, dve_rl, dve_x1 = (
            sem(n) for n in ("pe_shift", "act_exp", "pe_pv", "dve_rl", "dve_x1"))
        dve_st2, dve_mv2, pool_ve2, pool_rstd2, pool_sh2 = (
            sem(n) for n in ("dve_st2", "dve_mv2", "pool_ve2", "pool_rstd2", "pool_sh2"))
        act_xn2, pe_h2T, act_h2T, dve_d, dve_xk, dve_xr = (
            sem(n) for n in ("act_xn2", "pe_h2T", "act_h2T", "dve_d", "dve_xk", "dve_xr"))
        pe_k, act_relu, act_ka, pool_wv, pe_r, act_tanh, pe_v, dve_gv, pool_y, dve_y, stored = (
            sem(n) for n in ("pe_k", "act_relu", "act_ka", "pool_wv", "pe_r", "act_tanh", "pe_v",
                             "dve_gv", "pool_y", "dve_y", "stored"))

        def blk(j):
            return slice(j * P, (j + 1) * P)

        def blocks(h):
            return range(2 * h, 2 * h + 2)

        def half(h):
            return slice(h * H, (h + 1) * H)

        def at_least(eng, s, value):
            if value > 0:
                eng.wait_ge(s, value)

        LAST = B - 1
        STEPS = range(-1, B)

        def is_mixed(b):
            return 0 <= b < LAST

        block = ctx.enter_context(nc.Block())

        @block.sync
        def _(sp):
            def tokens(dram, b, js):
                return dram[b].rearrange("(j p) d -> p j d", p=P)[:, js.start:js.stop]

            for h in range(2):
                sp.dma_start(xs[:, 0, 2 * h:2 * h + 2], tokens(x, 0, blocks(h))).then_inc(x0_in[h], 16)
            sp.dma_start(wa[:], attn_w).then_inc(wa_in, 16)
            for n, v in enumerate((attn_b, mu_r, mu_k)):
                sp.dma_start(vecs[:, n:n + 1], v.rearrange("(p a) -> p a", a=1)).then_inc(wa_in, 16)
            for n, dram in enumerate((w_r, w_k, w_v)):
                sp.dma_start(ffn_w[:, n], dram).then_inc(w_in, 16)
            sp.dma_start(xs[:, 1], tokens(x, 1, range(NT))).then_inc(x1_in, 16)
            sp.dma_start(xs[:, 2], tokens(x, 2, range(NT))).then_inc(x2_in, 16)
            sp.wait_ge(dve_gate, 6)
            sp.dma_start(gate_dram, gate[:].rearrange("b g d -> b (g d)")).then_inc(gate_out, 16)
            sp.wait_ge(gate_out, 16)
            sp.dma_start(gates[:].rearrange("p b g d -> p (b g d)"),
                         gate_dram.rearrange("(a b) n -> a (b n)", a=1).to_broadcast([P, 2 * B * D])).then_inc(gates_in, 16)
            for b in range(3, B):
                sp.dma_start(xs[:, b], tokens(x, b, range(NT))).then_inc(x_rest_in, 16)
            for b in range(LAST):
                sp.wait_ge(pool_y, b + 1)
                sp.dma_start(tokens(out, b, range(NT)), ys[:, b]).then_inc(stored, 16)
            for h in range(2):
                sp.wait_ge(dve_y, h + 1)
                sp.dma_start(tokens(out, LAST, blocks(h)), ys[:, LAST, 2 * h:2 * h + 2]).then_inc(stored, 16)
            sp.wait_ge(stored, 16 * (B + 1))

        @block.gpsimd
        def _(pool):
            pool.memset(ident[:], 0.0).then_inc(pool_ident, 1)
            pool.wait_ge(pool_ident, 1)
            pool.affine_select(out=ident[:], in_=ident[:], compare_op=ALU.not_equal, fill=1.0,
                               base=0, pattern=[[-1, P]], channel_multiplier=1).then_inc(pool_ident, 1)
            pool.iota(offs[:], pattern=[[1, WIDE]], base=-(NT - 1) * P, channel_multiplier=-1).then_inc(pool_offs, 1)

            def rstd(js, n, mv, ve, nm, rs, sh, s_mv, s_ve, s_rstd, s_sh):
                js = slice(js.start, js.stop)
                pool.wait_ge(s_mv, n + 1)
                pool.tensor_scalar(ve[:, js], mv[:, js, 1], EPS, 1.0, ALU.add, ALU.mult).then_inc(s_ve, 1)
                pool.tensor_scalar(nm[:, js], mv[:, js, 0], -1.0, 0.0, ALU.mult, ALU.add).then_inc(s_ve, 1)
                pool.wait_ge(s_ve, 2 * n + 2)
                pool.tensor_tensor(rs[:, js], ve[:, js], neg_half[:, js], ALU.pow).then_inc(s_rstd, 1)
                pool.wait_ge(s_rstd, n + 1)
                pool.tensor_tensor(sh[:, js], nm[:, js], rs[:, js], ALU.mult).then_inc(s_sh, 1)

            def rstd1_of(js, n):
                rstd(js, n, mv1, ve1, nm1, rstd1, sh1, dve_mv1, pool_ve1, pool_rstd1, pool_sh1)

            def rstd2_of(b):
                at_least(pool, act_xn2, 2 * b)
                for h in range(2):
                    rstd(blocks(h), 2 * b + h, mv2, ve2, nm2, rstd2, sh2, dve_mv2, pool_ve2, pool_rstd2, pool_sh2)

            def gated_wv(b):
                if b == 0:
                    pool.wait_ge(gates_in, 16)
                    pool.wait_ge(act_wT, 1)
                at_least(pool, pe_v, b)
                pool.tensor_tensor(wv_g[:], wvT, gates[:, b, 1], ALU.mult).then_inc(pool_wv, 1)

            def add_mix(b):
                pool.wait_ge(dve_gv, b + 1)
                pool.tensor_tensor(ys[:, b], xs[:, b], gv[:].rearrange("p (j d) -> p j d", j=NT),
                                   ALU.add).then_inc(pool_y, 1)

            pool.wait_ge(dve_const, 2)
            for h in range(2):
                rstd1_of(blocks(h), h)
            for t in STEPS:
                if is_mixed(t - 2):
                    gated_wv(t - 2)
                if t + 2 < B:
                    if t + 2 > 1:
                        pool.wait_ge(act_xn, t + 3)
                    else:
                        pool.wait_ge(act_xn, 2)
                    rstd1_of(range(NT), t + 3)
                if is_mixed(t - 2):
                    add_mix(t - 2)
                if 0 < t + 1 < B:
                    pool.wait_ge(act_fT_hi, t + 3)
                    pool.wait_ge(pe_scores, NT * (t + 1))
                    pool.tensor_tensor(fT_lo[:], fT[:], fT_hi[:].bitcast(F32), ALU.subtract).then_inc(pool_fT_lo, 1)
                if t == LAST:
                    gated_wv(LAST - 1)
                if 0 <= t:
                    rstd2_of(t)
            gated_wv(LAST)
            add_mix(LAST - 1)

        @block.scalar
        def _(act):
            act.dma_start(c_sb[:], cond).then_inc(c_in, 16)
            act.dma_start(wm[:], wmod).then_inc(wmod_in, 16)

            def normalize(dst, b, js, rs, sh, done):
                for j in js:
                    ins = act.activation(dst[:, j], xs[:, b, j], ACT.Identity, scale=rs[:, j:j + 1],
                                         bias=sh[:, j:j + 1])
                ins.then_inc(done, 1)

            def modulate(dst, src, b, m, done):
                act.activation(dst, src, ACT.Identity, scale=modT[:, b, m + 1:m + 2],
                               bias=modT[:, b, m:m + 1]).then_inc(done, 1)

            def f_parts(dst, hi, src):
                act.activation(dst, src, ACT.Identity, bias=b_col).then_inc(act_fT, 1)
                act.activation(hi, src, ACT.Identity, bias=b_col).then_inc(act_fT_hi, 1)

            def exp(t, i):
                act.wait_ge(pe_shift, NT * t + i + 1)
                act.activation(pT[:, i], E[i][:], ACT.Exp).then_inc(act_exp, 1)

            def squared_relu(n, cols, src):
                act.wait_ge(pe_k, n + 1)
                act.activation(krT[:, cols], src, ACT.Relu).then_inc(act_relu, 1)
                act.wait_ge(act_relu, n + 1)
                at_least(act, pe_v, min(n, LAST))
                act.activation(kaT[:, cols], krT[:, cols], ACT.Square).then_inc(act_ka, 1)

            def tanh(n, cols, src):
                act.wait_ge(pe_r, n + 1)
                at_least(act, dve_gv, min(n, LAST))
                act.activation(th_r[:, cols], src, ACT.Tanh, scale=0.5).then_inc(act_tanh, 1)

            act.wait_ge(pe_cT, 1)
            act.activation(th_c[:], A[:, 0:B], ACT.Tanh, scale=0.5).then_inc(act_cT, 1)
            act.copy(cT[:], A[:, 0:B]).then_inc(act_cT, 1)
            act.wait_ge(pool_offs, 1)
            act.activation(absd[:], offs[:], ACT.Abs).then_inc(act_absd, 1)
            for h in range(2):
                act.wait_ge(pool_sh1, h + 1)
                normalize(xn, 0, blocks(h), rstd1, sh1, act_xn)
            act.wait_ge(dve_mod, 1)
            for h in range(2):
                act.wait_ge(pe_xnT, h + 1)
                modulate(hT[:, half(h)], E[h][:, 0:H], 0, 0, act_hT)
            act.wait_ge(wa_in, 64)
            for h in range(2):
                act.wait_ge(pe_fT, h + 1)
                f_parts(fT[:, half(h)], fT_hi[:, half(h)], E[2 + h][:, 0:H])
            act.wait_ge(pe_wT, 1)
            act.copy(ffn_wT[:], C[:, 0:3 * P].rearrange("p (n d) -> p n d", n=3)).then_inc(act_wT, 1)

            for t in STEPS:
                if is_mixed(t - 2):
                    tanh(t - 2, slice(0, S), C[:])
                if 0 <= t:
                    act.wait_ge(pe_nmx, t + 1)
                    act.copy(nmx_row[:], O[0][0:2, :]).then_inc(act_nmx, 1)
                if 0 < t + 1 < B:
                    act.wait_ge(pe_xnT, t + 3)
                    act.wait_ge(pe_fT, t + 2)
                    modulate(hT[:], O[1][:], t + 1, 0, act_hT)
                if 0 <= t:
                    at_least(act, pe_pv, 2 * t)
                    exp(t, 0)
                    exp(t, 1)
                if is_mixed(t - 1):
                    act.wait_ge(pe_h2T, t)
                    at_least(act, dve_xr, t - 1)
                    modulate(h2T[:, 1:S + 1], C[:], t - 1, 2, act_h2T)
                if 0 <= t:
                    exp(t, 2)
                    exp(t, 3)
                if 0 < t + 1 < B:
                    act.wait_ge(pe_fT, t + 3)
                    act.wait_ge(pe_ftok, t + 1)
                    if t == 0:
                        act.wait_ge(dve_fT_lo0, 2)
                    at_least(act, pool_fT_lo, t)
                    f_parts(fT[:], fT_hi[:], A[:])
                if t + 2 < B:
                    act.wait_ge(pool_sh1, t + 4)
                    act.wait_ge(pe_xnT, t + 3)
                    normalize(xn, t + 2, range(NT), rstd1, sh1, act_xn)
                if is_mixed(t - 1):
                    squared_relu(t - 1, slice(0, S), C[:])
                if 0 <= t < LAST:
                    at_least(act, pe_h2T, t)
                    for h in range(2):
                        act.wait_ge(pool_sh2, 2 * t + h + 1)
                        normalize(xn2, t, blocks(h), rstd2, sh2, act_xn2)
            act.wait_ge(pe_h2T, LAST)
            act.wait_ge(dve_xr, LAST)
            for h in range(2):
                act.wait_ge(pool_sh2, 2 * LAST + h + 1)
                normalize(xn2, LAST, blocks(h), rstd2, sh2, act_xn2)
                act.wait_ge(pe_h2T, LAST + h + 1)
                modulate(h2T[:, 1 + h * H:1 + (h + 1) * H], E[h][:, 0:H], LAST, 2, act_h2T)
                if h == 0:
                    tanh(LAST - 1, slice(0, S), C[:])
            for h in range(2):
                squared_relu(LAST + h, half(h), E[2 + h][:, 0:H])
                tanh(LAST + h, half(h), E[h][:, 0:H])

        @block.vector
        def _(dve):
            dve.memset(neg_half[:], -0.5).then_inc(dve_const, 1)
            dve.memset(h2T[:, 0:1], 0.0).then_inc(dve_const, 1)
            dve.memset(ones_r[:].bitcast(F32), 1.0).then_inc(dve_const, 1)
            dve.memset(ftok[:, :, D:D + 1], 1.0).then_inc(dve_const, 1)
            dve.wait_ge(pool_ident, 2)
            dve.tensor_copy(ident_r[:], ident[:]).then_inc(dve_const, 1)

            def stats(b, js, st, mv, s_st, s_mv, seen):
                for j in js:
                    dve.bn_stats(st[:, j], xs[:, b, j]).then_inc(s_st, 1)
                for n, j in enumerate(js):
                    dve.wait_ge(s_st, seen + n + 1)
                    ins = dve.bn_aggr(mv[:, j], st[:, j])
                ins.then_inc(s_mv, 1)

            def stats1(b):
                if b == 0:
                    for h in range(2):
                        dve.wait_ge(x0_in[h], 16)
                        stats(0, blocks(h), st1, mv1, dve_st1, dve_mv1, 2 * h)
                    return
                if b <= 3:
                    dve.wait_ge((x1_in, x2_in, x_rest_in)[b - 1], 16 if b < 3 else 16 * (B - 3))
                dve.wait_ge(pool_ve1, 2 * b + 2)
                dve.wait_ge(dve_mv1, b + 1)
                stats(b, range(NT), st1, mv1, dve_st1, dve_mv1, NT * b)

            def mixed_tokens(n, cols, prev):
                dve.wait_ge(act_h2T, n + 1)
                at_least(dve, dve_xr, n)
                nxt = slice(prev.start + 1, prev.stop + 1)
                dve.tensor_tensor(dT[:, cols], h2T[:, nxt], h2T[:, prev], ALU.subtract).then_inc(dve_d, 1)
                dve.wait_ge(dve_d, n + 1)
                at_least(dve, pe_k, min(n, LAST))
                dve.scalar_tensor_tensor(xkT[:, cols], dT[:, cols], mu_k_col, h2T[:, prev], ALU.mult,
                                         ALU.add).then_inc(dve_xk, 1)
                at_least(dve, pe_r, min(n, LAST))
                dve.scalar_tensor_tensor(xrT[:, cols], dT[:, cols], mu_r_col, h2T[:, prev], ALU.mult,
                                         ALU.add).then_inc(dve_xr, 1)

            def gated_v(n, cols, src):
                dve.wait_ge(pe_v, n + 1)
                dve.wait_ge(act_tanh, n + 1)
                at_least(dve, pool_y, min(n, LAST))
                dve.scalar_tensor_tensor(gv[:, cols], th_r[:, cols], 1.0, src, ALU.add, ALU.mult).then_inc(dve_gv, 1)

            stats1(0)
            dve.wait_ge(act_cT, 2)
            dve.scalar_tensor_tensor(silu2[:], th_c[:], 1.0, cT[:], ALU.add, ALU.mult).then_inc(dve_silu, 1)
            dve.wait_ge(dve_silu, 1)
            dve.tensor_scalar(silu[:], silu2[:], 0.5, None, ALU.mult).then_inc(dve_silu, 1)
            dve.wait_ge(act_absd, 1)
            dve.tensor_scalar(bias[:], absd[:], float(MAX_DISTANCE), SCALE, ALU.min, ALU.mult).then_inc(dve_bias, 1)
            dve.wait_ge(pe_mod, 1)
            md = O[1][:, 0:4 * B].rearrange("p (m b) -> p b m", m=4)
            dve.tensor_copy(modT[:, :, 0:4:2], md[:, :, 0:4:2])
            dve.tensor_scalar(modT[:, :, 1:4:2], md[:, :, 1:4:2], 1.0, None, ALU.add).then_inc(dve_mod, 1)
            dve.wait_ge(pe_gate, 1)
            dve.tensor_copy(gate_raw[:], O[0][0:B, 0:2 * D].rearrange("b (g d) -> b g d", g=2)).then_inc(dve_gate, 1)
            dve.wait_ge(dve_gate, 1)
            dve.tensor_scalar(gate_two[:], gate_raw[:], 0.0, 2.0, ALU.is_ge, ALU.mult).then_inc(dve_gate, 1)
            dve.wait_ge(dve_gate, 2)
            dve.tensor_scalar(gate_sign[:], gate_two[:], -1.0, None, ALU.add).then_inc(dve_gate, 1)
            dve.wait_ge(dve_gate, 3)
            dve.tensor_tensor(gate_abs[:], gate_raw[:], gate_sign[:], ALU.mult).then_inc(dve_gate, 1)
            dve.wait_ge(dve_gate, 4)
            dve.tensor_scalar(gate_half[:], gate_abs[:, 1], GATE_MIN, 0.5, ALU.max, ALU.mult).then_inc(dve_gate, 1)
            dve.scalar_tensor_tensor(gate[:, 0], gate_abs[:, 0], GATE_MIN, gate_sign[:, 0], ALU.max, ALU.mult)
            dve.wait_ge(dve_gate, 5)
            dve.tensor_tensor(gate[:, 1], gate_half[:], gate_sign[:, 1], ALU.mult).then_inc(dve_gate, 1)
            for h in range(2):
                dve.wait_ge(act_fT_hi, h + 1)
                dve.tensor_tensor(fT_lo[:, half(h)], fT[:, half(h)], fT_hi[:, half(h)].bitcast(F32),
                                  ALU.subtract).then_inc(dve_fT_lo0, 1)
            stats1(1)

            for t in STEPS:
                if 0 <= t:
                    at_least(dve, dve_nmx, t)
                    if t == 0:
                        dve.wait_ge(dve_bias, 1)
                    for i in range(NT):
                        dve.wait_ge(pe_scores, NT * t + i + 1)
                        dve.tensor_tensor_reduce(E[i][:], E[i][:], bias[:, (NT - 1 - i) * P:(NT - 1 - i) * P + S],
                                                 1.0, LOWEST, ALU.add, ALU.max, mx[:, i:i + 1]).then_inc(dve_max, 1)
                    dve.wait_ge(dve_max, NT * (t + 1))
                    at_least(dve, pe_nmx, t)
                    dve.tensor_scalar(nmx[:, :, 0], mx[:], -1.0, None, ALU.mult).then_inc(dve_nmx_hi, 1)
                    dve.wait_ge(dve_nmx_hi, t + 1)
                    dve.scalar_tensor_tensor(nmx[:, :, 1], mx[:], -1.0, nmx[:, :, 0].bitcast(F32), ALU.mult,
                                             ALU.subtract).then_inc(dve_nmx, 1)
                    if t == 0:
                        dve.wait_ge(gates_in, 16)
                    dve.wait_ge(pe_ftok, t + 1)
                    at_least(dve, pe_pv, 2 * t)
                    dve.tensor_tensor(ftok[:, :, 0:D], A[:].rearrange("p (j d) -> p j d", j=NT),
                                      gates[:, t, 0:1].to_broadcast([P, NT, D]), ALU.mult).then_inc(dve_ftok, 1)
                if 1 < t + 2 < B:
                    stats1(t + 2)
                if is_mixed(t - 2):
                    gated_v(t - 2, slice(0, S), C[:])
                if is_mixed(t - 1):
                    mixed_tokens(t - 1, slice(0, S), slice(0, S))
                if 0 <= t:
                    at_least(dve, dve_x1, NT * t)
                    at_least(dve, pool_ve2, 4 * t)
                    at_least(dve, dve_mv2, 2 * t)
                    for h in range(2):
                        ob = O[h][:, 0:2 * (D + 1)].rearrange("p (j d) -> p j d", j=2)
                        dve.wait_ge(pe_pv, 2 * t + h + 1)
                        dve.reciprocal(rl[:, 2 * h:2 * h + 2], ob[:, :, D]).then_inc(dve_rl, 1)
                        dve.wait_ge(dve_rl, 2 * t + h + 1)
                        for j in range(2):
                            n = 2 * h + j
                            dve.scalar_tensor_tensor(xs[:, t, n], ob[:, j, 0:D], rl[:, n:n + 1], xs[:, t, n],
                                                     ALU.mult, ALU.add).then_inc(dve_x1, 1)
                        dve.wait_ge(dve_x1, NT * t + 2 * h + 2)
                        stats(t, blocks(h), st2, mv2, dve_st2, dve_mv2, NT * t + 2 * h)
            mixed_tokens(LAST, half(0), half(0))
            gated_v(LAST - 1, slice(0, S), C[:])
            mixed_tokens(LAST + 1, half(1), half(1))
            for h in range(2):
                gated_v(LAST + h, half(h), E[2 + h][:, 0:H])
                dve.wait_ge(dve_gv, LAST + h + 1)
                dve.tensor_tensor(ys[:, LAST, 2 * h:2 * h + 2], xs[:, LAST, 2 * h:2 * h + 2],
                                  gv[:, half(h)].rearrange("p (j d) -> p j d", j=2), ALU.add).then_inc(dve_y, 1)

        @block.tensor
        def _(pe):
            def keep_warm(n):
                for _ in range(n):
                    pe.matmul(A[:, 0:P], ident[:], ident[:], start=True, stop=True)

            def each_block(js, dst, lhsT, rhs, done, transposed=False):
                for j in js:
                    if transposed:
                        mm = pe.transpose(dst(j), lhsT(j), rhs)
                    else:
                        mm = pe.matmul(dst(j), lhsT(j), rhs, start=True, stop=True)
                mm.then_inc(done, 1)

            pe.wait_ge(pool_ident, 2)
            keep_warm(WARM[0])
            pe.wait_ge(c_in, 16)
            pe.transpose(A[:, 0:B], c_sb[:], ident[0:B, 0:B]).then_inc(pe_cT, 1)
            pe.wait_ge(act_cT, 2)
            keep_warm(WARM[1])
            pe.wait_ge(dve_silu, 2)
            pe.wait_ge(wmod_in, 16)
            wm6 = wm[:].rearrange("p (m d) -> p m d", m=6)
            for n, m in enumerate((0, 1, 3, 4)):
                mm = pe.matmul(O[1][:, n * B:(n + 1) * B], wm6[:, m], silu[:], start=True, stop=True)
            mm.then_inc(pe_mod, 1)
            for h in range(2):
                pe.wait_ge(act_xn, h + 1)
                each_block(blocks(h), lambda j: E[h][:, blk(j % 2)], lambda j: xn[:, j], ident[:], pe_xnT, True)
            pe.matmul(O[0][0:B, 0:2 * D].rearrange("b (g d) -> b g d", g=2), silu[:], wm6[:, 2:6:3],
                      start=True, stop=True).then_inc(pe_gate, 1)
            pe.wait_ge(w_in, 48)
            each_block(range(3), lambda n: C[:, blk(n)], lambda n: ffn_w[:, n], ident[:], pe_wT, True)
            pe.wait_ge(wa_in, 64)
            for h in range(2):
                pe.wait_ge(act_hT, h + 1)
                pe.matmul(E[2 + h][:, 0:H], wa[:], hT[:, half(h)], start=True, stop=True).then_inc(pe_fT, 1)
            keep_warm(WARM[2])

            for t in STEPS:
                if 0 <= t:
                    if t == 0:
                        pe.wait_ge(dve_fT_lo0, 2)
                    at_least(pe, pool_fT_lo, t)
                    for i in range(NT):
                        at_least(pe, act_exp, NT * (t - 1) + i + 1)
                        pe.matmul(E[i][:], fT_lo[:, blk(i)], fT_hi[:], start=True, stop=False)
                        pe.matmul(E[i][:], fT_hi[:, blk(i)], fT_lo[:], start=False, stop=False)
                        pe.matmul(E[i][:], fT_hi[:, blk(i)], fT_hi[:], start=False, stop=True).then_inc(pe_scores, 1)
                if is_mixed(t - 2):
                    pe.wait_ge(dve_xr, t - 1)
                    pe.wait_ge(act_relu, t - 1)
                    each_block(range(NT), lambda j: C[:, blk(j)], lambda j: xrT[:, blk(j)], wrT, pe_r)
                if 0 <= t:
                    each_block(range(NT), lambda j: A[:, blk(j)], lambda j: fT[:, blk(j)], ident[:], pe_ftok, True)
                    pe.wait_ge(dve_nmx, t + 1)
                    at_least(pe, dve_x1, NT * t)
                    each_block(range(NT), lambda j: O[0][0:2, blk(j)].bitcast(F32R), lambda j: nmx[:, j],
                               ident_r[:], pe_nmx, True)
                if 0 < t + 1 < B:
                    pe.wait_ge(act_xn, t + 3)
                    each_block(range(NT), lambda j: O[1][:, blk(j)], lambda j: xn[:, j], ident[:], pe_xnT, True)
                if is_mixed(t - 2):
                    pe.wait_ge(act_tanh, t - 1)
                    pe.wait_ge(act_ka, t - 1)
                    pe.wait_ge(pool_wv, t - 1)
                    each_block(range(NT), lambda j: C[:, blk(j)], lambda j: kaT[:, blk(j)], wv_g[:], pe_v)
                if 0 <= t:
                    pe.wait_ge(act_nmx, t + 1)
                    for i in range(NT):
                        pe.matmul(E[i][:], ones_r[:], nmx_row[:], start=False, stop=True,
                                  skip_group_check=True).then_inc(pe_shift, 1)
                if is_mixed(t - 1):
                    pe.wait_ge(act_xn2, 2 * t)
                    at_least(pe, dve_gv, t - 1)
                    if t == 1:
                        pe.wait_ge(act_wT, 1)
                    each_block(range(NT), lambda j: C[:, blk(j)], lambda j: xn2[:, j], ident[:], pe_h2T, True)
                if 0 < t + 1 < B:
                    pe.wait_ge(act_hT, t + 3)
                    pe.wait_ge(dve_ftok, t + 1)
                    pe.matmul(A[:], wa[:], hT[:], start=True, stop=True).then_inc(pe_fT, 1)
                if 0 <= t:
                    pe.wait_ge(dve_ftok, t + 1)
                    for h in range(2):
                        for k in range(NT):
                            if h == 0:
                                pe.wait_ge(act_exp, NT * t + k + 1)
                            for j in range(2):
                                mm = pe.matmul(O[h][:, j * (D + 1):(j + 1) * (D + 1)], pT[:, k, blk(2 * h + j)],
                                               ftok[:, k], start=(k == 0 and j == 0), stop=(k == NT - 1),
                                               skip_group_check=True)
                        mm.then_inc(pe_pv, 1)
                if is_mixed(t - 1):
                    pe.wait_ge(dve_xk, t)
                    pe.wait_ge(act_h2T, t)
                    pe.matmul(C[:], wkT, xkT[:], start=True, stop=True).then_inc(pe_k, 1)

            def last_h2T(h):
                pe.wait_ge(act_xn2, 2 * LAST + h + 1)
                each_block(blocks(h), lambda j: E[h][:, blk(j % 2)], lambda j: xn2[:, j], ident[:], pe_h2T, True)

            def last_k(h):
                pe.wait_ge(dve_xk, LAST + h + 1)
                pe.matmul(E[2 + h][:, 0:H], wkT, xkT[:, half(h)], start=True, stop=True).then_inc(pe_k, 1)

            def last_r(h):
                pe.wait_ge(dve_xr, LAST + h + 1)
                pe.wait_ge(act_h2T, LAST + h + 1)
                each_block(blocks(h), lambda j: E[h][:, blk(j % 2)], lambda j: xrT[:, blk(j)], wrT, pe_r)

            def last_v(h):
                pe.wait_ge(act_ka, LAST + h + 1)
                pe.wait_ge(pool_wv, LAST + 1)
                each_block(blocks(h), lambda j: E[2 + h][:, blk(j % 2)], lambda j: kaT[:, blk(j)], wv_g[:], pe_v)

            pe.wait_ge(dve_xr, LAST)
            pe.wait_ge(act_relu, LAST)
            each_block(range(NT), lambda j: C[:, blk(j)], lambda j: xrT[:, blk(j)], wrT, pe_r)
            last_h2T(0)
            pe.wait_ge(act_tanh, LAST)
            pe.wait_ge(act_ka, LAST)
            pe.wait_ge(pool_wv, LAST)
            each_block(range(NT), lambda j: C[:, blk(j)], lambda j: kaT[:, blk(j)], wv_g[:], pe_v)
            last_h2T(1)
            last_k(0)
            last_r(0)
            last_k(1)
            last_v(0)
            last_r(1)
            last_v(1)


_INS = ["L0_attn_x", "L0_attn_W", "L0_attn_b", "L0_ffn_W_r", "L0_ffn_W_k", "L0_ffn_W_v", "L0_ffn_mu_r",
        "L0_ffn_mu_k", "L0_c", "L0_wmod"]
_OUTS = [((8, 512, 128), "float32")]


def kernel(**inputs):
    import numpy as _np
    import concourse.bacc as _bacc
    from concourse import mybir as _mybir
    from concourse.bass_utils import run_bass_kernel_spmd as _run

    nc = _bacc.Bacc("TRN2", target_bir_lowering=False, num_devices=1)
    arrays, args = {}, []
    for name in _INS:
        a = _np.ascontiguousarray(inputs[name])
        arrays[f"in_{name}_dram"] = a
        args.append(nc.dram_tensor(f"in_{name}_dram", a.shape, _mybir.dt.from_np(a.dtype), kind="ExternalInput").ap())
    for i, (shape, dtype) in enumerate(_OUTS):
        dt = _mybir.dt.from_np(_np.dtype(dtype))
        args.append(nc.dram_tensor(f"out_{i}_dram", shape, dt, kind="ExternalOutput").ap())
    adaln_attention_channelmix_kernel(nc, *args)
    r = _run(nc, [arrays], core_ids=[0])
    return r.results[0]["out_0_dram"]
```

```python
from contextlib import ExitStack

import concourse.bass as bass
from concourse import mybir

ALU = mybir.AluOpType
ACT = mybir.ActivationFunctionType
F32 = mybir.dt.float32
F32R = mybir.dt.float32r
I32 = mybir.dt.int32

P = 128
EPS = 1e-5
MAX_DISTANCE = 10
SCALE = 0.01
GATE_MIN = 0.25
LOWEST = -3.0e38
WARM_C, WARM_MOD, WARM_STEP_1, WARM_LAST = 3, 2, 5, 1


def adaln_attention_channelmix_kernel(
    nc: bass.Bass,
    x: bass.AP,
    attn_w: bass.AP,
    attn_b: bass.AP,
    w_r: bass.AP,
    w_k: bass.AP,
    w_v: bass.AP,
    mu_r: bass.AP,
    mu_k: bass.AP,
    cond: bass.AP,
    wmod: bass.AP,
    out: bass.AP,
):
    B, S, D = x.shape
    NT = S // P
    H = S // 2
    WIDE = (2 * NT - 1) * P
    assert D == P and S == NT * P and NT == 4

    with ExitStack() as ctx:
        def sb(name, shape, dt=F32):
            return ctx.enter_context(nc.sbuf_tensor(name, shape, dt))

        def bank(name):
            return ctx.enter_context(nc.psum_tensor(name, [P, 512], F32))

        def sem(name):
            return ctx.enter_context(nc.semaphore(name))

        ident = sb("ident", [P, P])
        ident_r = sb("ident_r", [P, P], F32R)
        ones_r = sb("ones_r", [2, P], F32R)
        one_row = sb("one_row", [1, P])
        offs = sb("offs", [P, WIDE], I32)
        absd = sb("absd", [P, WIDE])
        bias = sb("bias", [P, WIDE])
        neg_half = sb("neg_half", [P, NT])
        wa = sb("wa", [P, D])
        ffn_w = sb("ffn_w", [P, 3, D])
        ffn_wT = sb("ffn_wT", [P, 3, D])
        wrT, wkT, wvT = (ffn_wT[:, n] for n in range(3))
        vecs = sb("vecs", [P, 3])
        b_col, mu_r_col, mu_k_col = (vecs[:, n:n + 1] for n in range(3))
        c_sb = sb("c_sb", [B, D])
        wm = sb("wm", [P, 6 * D])
        th_c = sb("th_c", [P, B])
        silu2 = sb("silu2", [P, B])
        silu = sb("silu", [P, B])
        modT = sb("modT", [P, B, 4])
        half_sign = sb("half_sign", [B, 2, D])
        gate_abs = sb("gate_abs", [B, 2, D])
        gate = sb("gate", [B, 2, D])
        gates = sb("gates", [P, B, 2, D])
        gate_dram = nc.dram_tensor("gate_dram", (B, 2 * D), F32).ap()
        xs = sb("xs", [P, B, NT, D])
        ys = sb("ys", [P, B, NT, D])
        st1, mv1, ve1, nm1, rstd1, sh1 = (
            sb(n, [P, NT] + d) for n, d in (("st1", [6]), ("mv1", [2]), ("ve1", []), ("nm1", []),
                                            ("rstd1", []), ("sh1", [])))
        st2, mv2, ve2, nm2, rstd2, sh2 = (
            sb(n, [P, NT] + d) for n, d in (("st2", [6]), ("mv2", [2]), ("ve2", []), ("nm2", []),
                                            ("rstd2", []), ("sh2", [])))
        xn = sb("xn", [P, NT, D])
        hT = sb("hT", [P, S])
        fT = sb("fT", [P, S])
        fT_hi = sb("fT_hi", [P, S], F32R)
        fT_lo = sb("fT_lo", [P, S], F32R)
        ftok = sb("ftok", [P, NT, D + 1])
        mx = sb("mx", [P, NT])
        nmx = sb("nmx", [P, NT, 2], F32R)
        nmx_row = sb("nmx_row", [2, S], F32R)
        pT = sb("pT", [P, NT, S])
        rl = sb("rl", [P, NT])
        xn2 = sb("xn2", [P, NT, D])
        h2T = sb("h2T", [P, S + 1])
        dT = sb("dT", [P, S])
        xkT = sb("xkT", [P, S])
        xrT = sb("xrT", [P, S])
        krT = sb("krT", [P, S])
        kaT = sb("kaT", [P, S])
        wv_g = sb("wv_g", [P, D])
        th_r = sb("th_r", [P, S])
        gv = sb("gv", [P, S])
        last_th_r = sb("last_th_r", [P, S])
        last_gv = sb("last_gv", [P, S])

        E = [bank(f"scores{i}") for i in range(NT)]
        O = [bank(f"pv{i}") for i in range(2)]
        A = bank("bank_a")
        C = bank("bank_c")

        x0_in = [sem(f"x0_in{h}") for h in range(2)]
        x1_in, x2_in, x_rest_in, c_in, wmod_a_in, wmod_in, wa_in, w_in = (
            sem(n) for n in ("x1_in", "x2_in", "x_rest_in", "c_in", "wmod_a_in", "wmod_in", "wa_in", "w_in"))
        pool_ident, pool_offs, act_absd, dve_const, dve_bias = (
            sem(n) for n in ("pool_ident", "pool_offs", "act_absd", "dve_const", "dve_bias"))
        pe_cT, act_cT, dve_silu, pe_mod, dve_mod, pe_wT, act_wT = (
            sem(n) for n in ("pe_cT", "act_cT", "dve_silu", "pe_mod", "dve_mod", "pe_wT", "act_wT"))
        pe_gate, act_gate_abs, dve_half_sign, dve_gate, pe_gate0, act_gate0, gate_out, gates_in = (
            sem(n) for n in ("pe_gate", "act_gate_abs", "dve_half_sign", "dve_gate", "pe_gate0", "act_gate0",
                             "gate_out", "gates_in"))
        dve_st1, dve_mv1, dve_xn0, pool_ve1, pool_rstd1, pool_sh1 = (
            sem(n) for n in ("dve_st1", "dve_mv1", "dve_xn0", "pool_ve1", "pool_rstd1", "pool_sh1"))
        act_xn, pe_xnT, act_hT, pe_fT, act_fT, act_fT_hi, pool_fT_lo, dve_fT_lo0 = (
            sem(n) for n in ("act_xn", "pe_xnT", "act_hT", "pe_fT", "act_fT", "act_fT_hi", "pool_fT_lo",
                             "dve_fT_lo0"))
        pe_ftok, dve_ftok, pe_scores, dve_max, dve_nmx_hi, dve_nmx, pe_nmx, act_nmx = (
            sem(n) for n in ("pe_ftok", "dve_ftok", "pe_scores", "dve_max", "dve_nmx_hi", "dve_nmx",
                             "pe_nmx", "act_nmx"))
        pe_shift, act_exp, pe_pv, dve_rl, dve_x1 = (
            sem(n) for n in ("pe_shift", "act_exp", "pe_pv", "dve_rl", "dve_x1"))
        dve_st2, dve_mv2, dve_last_xn2, pool_ve2, pool_rstd2, pool_sh2 = (
            sem(n) for n in ("dve_st2", "dve_mv2", "dve_last_xn2", "pool_ve2", "pool_rstd2", "pool_sh2"))
        act_xn2, pe_h2T, act_h2T, dve_d, dve_xk, dve_xr = (
            sem(n) for n in ("act_xn2", "pe_h2T", "act_h2T", "dve_d", "dve_xk", "dve_xr"))
        pe_k, act_relu, act_ka, pool_wv, pe_r, act_tanh, pe_v, dve_gv, pool_y, dve_y, stored = (
            sem(n) for n in ("pe_k", "act_relu", "act_ka", "pool_wv", "pe_r", "act_tanh", "pe_v",
                             "dve_gv", "pool_y", "dve_y", "stored"))

        def blk(j):
            return slice(j * P, (j + 1) * P)

        def blocks(h):
            return range(2 * h, 2 * h + 2)

        def half(h):
            return slice(h * H, (h + 1) * H)

        def at_least(eng, s, value):
            if value > 0:
                eng.wait_ge(s, value)

        LAST = B - 1
        STEPS = range(-1, B)

        def is_mixed(b):
            return 0 <= b < LAST

        def h2T_bank(b):
            return C if b < LAST - 1 else O[1]

        def kv_bank(b):
            return C if b < LAST - 1 else E[3]

        def r_bank(b):
            return C if b < LAST - 1 else E[2]

        block = ctx.enter_context(nc.Block())

        @block.sync
        def _(sp):
            def tokens(dram, b, js):
                return dram[b].rearrange("(j p) d -> p j d", p=P)[:, js.start:js.stop]

            for h in range(2):
                sp.dma_start(xs[:, 0, 2 * h:2 * h + 2], tokens(x, 0, blocks(h))).then_inc(x0_in[h], 16)
            sp.dma_start(wm[:, 0:2 * D], wmod[:, 0:2 * D]).then_inc(wmod_a_in, 16)
            sp.dma_start(wm[:, 2 * D:], wmod[:, 2 * D:]).then_inc(wmod_in, 16)
            sp.dma_start(wa[:], attn_w).then_inc(wa_in, 16)
            sp.dma_start(b_col, attn_b.rearrange("(p a) -> p a", a=1)).then_inc(wa_in, 16)
            sp.dma_start(xs[:, 1], tokens(x, 1, range(NT))).then_inc(x1_in, 16)
            for n, dram in enumerate((w_r, w_k, w_v)):
                sp.dma_start(ffn_w[:, n], dram).then_inc(w_in, 16)
            for column, dram in ((mu_r_col, mu_r), (mu_k_col, mu_k)):
                sp.dma_start(column, dram.rearrange("(p a) -> p a", a=1)).then_inc(w_in, 16)
            sp.dma_start(xs[:, 2], tokens(x, 2, range(NT))).then_inc(x2_in, 16)
            sp.wait_ge(dve_gate, 2)
            sp.dma_start(gate_dram, gate[:].rearrange("b g d -> b (g d)")).then_inc(gate_out, 16)
            sp.wait_ge(gate_out, 16)
            sp.dma_start(gates[:, 1:].rearrange("p b g d -> p (b g d)"),
                         gate_dram[1:].rearrange("(a b) n -> a (b n)", a=1).to_broadcast(
                             [P, 2 * (B - 1) * D])).then_inc(gates_in, 16)
            for b in range(3, B):
                sp.dma_start(xs[:, b], tokens(x, b, range(NT))).then_inc(x_rest_in, 16)
            for b in range(LAST):
                sp.wait_ge(pool_y, b + 1)
                sp.dma_start(tokens(out, b, range(NT)), ys[:, b]).then_inc(stored, 16)
            for h in range(2):
                sp.wait_ge(dve_y, h + 1)
                sp.dma_start(tokens(out, LAST, blocks(h)), ys[:, LAST, 2 * h:2 * h + 2]).then_inc(stored, 16)
            sp.wait_ge(stored, 16 * (B + 1))

        @block.gpsimd
        def _(pool):
            pool.memset(ident[:], 0.0).then_inc(pool_ident, 1)
            pool.wait_ge(pool_ident, 1)
            pool.affine_select(out=ident[:], in_=ident[:], compare_op=ALU.not_equal, fill=1.0,
                               base=0, pattern=[[-1, P]], channel_multiplier=1).then_inc(pool_ident, 1)
            pool.iota(offs[:], pattern=[[1, WIDE]], base=-(NT - 1) * P, channel_multiplier=-1).then_inc(pool_offs, 1)

            def rstd_only(js, n, mv, ve, rs, s_mv, s_ve, ve_seen, s_rstd):
                js = slice(js.start, js.stop)
                pool.wait_ge(s_mv, n + 1)
                pool.tensor_scalar(ve[:, js], mv[:, js, 1], EPS, 1.0, ALU.add, ALU.mult).then_inc(s_ve, 1)
                pool.wait_ge(s_ve, ve_seen + 1)
                pool.tensor_tensor(rs[:, js], ve[:, js], neg_half[:, js], ALU.pow).then_inc(s_rstd, 1)

            def rstd(js, n, mv, ve, nm, rs, sh, s_mv, s_ve, ve_seen, s_rstd, s_sh):
                js = slice(js.start, js.stop)
                pool.wait_ge(s_mv, n + 1)
                pool.tensor_scalar(ve[:, js], mv[:, js, 1], EPS, 1.0, ALU.add, ALU.mult).then_inc(s_ve, 1)
                pool.tensor_scalar(nm[:, js], mv[:, js, 0], -1.0, 0.0, ALU.mult, ALU.add).then_inc(s_ve, 1)
                pool.wait_ge(s_ve, ve_seen + 2)
                pool.tensor_tensor(rs[:, js], ve[:, js], neg_half[:, js], ALU.pow).then_inc(s_rstd, 1)
                pool.wait_ge(s_rstd, n + 1)
                pool.tensor_tensor(sh[:, js], nm[:, js], rs[:, js], ALU.mult).then_inc(s_sh, 1)

            def rstd1_of(b):
                if b == 0:
                    for h in range(2):
                        rstd_only(blocks(h), h, mv1, ve1, rstd1, dve_mv1, pool_ve1, h, pool_rstd1)
                else:
                    rstd(range(NT), b + 1, mv1, ve1, nm1, rstd1, sh1, dve_mv1, pool_ve1, 2 * b, pool_rstd1, pool_sh1)

            def rstd2_of(b):
                at_least(pool, act_xn2, 2 * b)
                for n in (2 * b, 2 * b + 1):
                    if b < LAST:
                        rstd(blocks(n % 2), n, mv2, ve2, nm2, rstd2, sh2, dve_mv2, pool_ve2, 2 * n, pool_rstd2, pool_sh2)
                    else:
                        rstd_only(blocks(n % 2), n, mv2, ve2, rstd2, dve_mv2, pool_ve2, 2 * LAST + n, pool_rstd2)

            def gated_wv(b):
                if b == 0:
                    pool.wait_ge(act_gate0, 1)
                    pool.wait_ge(act_wT, 1)
                if b == 1:
                    pool.wait_ge(gates_in, 16)
                at_least(pool, pe_v, b)
                pool.tensor_tensor(wv_g[:], wvT, gates[:, b, 1], ALU.mult).then_inc(pool_wv, 1)

            def add_mix(b):
                pool.wait_ge(dve_gv, b + 1)
                pool.tensor_tensor(ys[:, b], xs[:, b], gv[:].rearrange("p (j d) -> p j d", j=NT),
                                   ALU.add).then_inc(pool_y, 1)

            pool.wait_ge(dve_const, 2)
            rstd1_of(0)
            for t in STEPS:
                if is_mixed(t - 2):
                    gated_wv(t - 2)
                if t + 2 < B:
                    if t + 2 == 1:
                        pool.wait_ge(dve_xn0, 2)
                    at_least(pool, act_xn, t + 1)
                    rstd1_of(t + 2)
                if t == LAST:
                    gated_wv(LAST - 1)
                if is_mixed(t - 2):
                    add_mix(t - 2)
                if 0 < t + 1 < B:
                    pool.wait_ge(act_fT_hi, t + 3)
                    pool.wait_ge(pe_scores, NT * (t + 1))
                    pool.tensor_tensor(fT_lo[:], fT[:], fT_hi[:].bitcast(F32), ALU.subtract).then_inc(pool_fT_lo, 1)
                if 0 <= t:
                    rstd2_of(t)
            gated_wv(LAST)
            add_mix(LAST - 1)

        @block.scalar
        def _(act):
            act.dma_start(c_sb[:], cond).then_inc(c_in, 16)

            def normalize(dst, b, js, rs, sh, done):
                for j in js:
                    ins = act.activation(dst[:, j], xs[:, b, j], ACT.Identity, scale=rs[:, j:j + 1],
                                         bias=sh[:, j:j + 1])
                ins.then_inc(done, 1)

            def modulate(dst, src, b, m, done):
                act.activation(dst, src, ACT.Identity, scale=modT[:, b, m + 1:m + 2],
                               bias=modT[:, b, m:m + 1]).then_inc(done, 1)

            def f_parts(dst, hi, src):
                act.activation(dst, src, ACT.Identity, bias=b_col).then_inc(act_fT, 1)
                act.activation(hi, src, ACT.Identity, bias=b_col).then_inc(act_fT_hi, 1)

            def exp(t, i):
                act.wait_ge(pe_shift, NT * t + i + 1)
                act.activation(pT[:, i], E[i][:], ACT.Exp).then_inc(act_exp, 1)

            def squared_relu(n, cols, src):
                act.wait_ge(pe_k, n + 1)
                act.activation(krT[:, cols], src, ACT.Relu).then_inc(act_relu, 1)
                act.wait_ge(act_relu, n + 1)
                at_least(act, pe_v, min(n, LAST))
                act.activation(kaT[:, cols], krT[:, cols], ACT.Square).then_inc(act_ka, 1)

            def tanh(n, cols, src):
                act.wait_ge(pe_r, n + 1)
                if n < LAST:
                    at_least(act, dve_gv, n)
                act.activation((th_r if n < LAST else last_th_r)[:, cols], src, ACT.Tanh,
                               scale=0.5).then_inc(act_tanh, 1)

            act.wait_ge(pe_cT, 1)
            act.activation(th_c[:], A[:, 0:B], ACT.Tanh, scale=0.5).then_inc(act_cT, 1)
            act.wait_ge(pool_offs, 1)
            act.activation(absd[:], offs[:], ACT.Abs).then_inc(act_absd, 1)
            act.wait_ge(dve_mod, 1)
            for h in range(2):
                act.wait_ge(pe_xnT, h + 1)
                modulate(hT[:, half(h)], E[h][:, 0:H], 0, 0, act_hT)
            act.wait_ge(wa_in, 32)
            for h in range(2):
                act.wait_ge(pe_fT, h + 1)
                act.activation(fT_hi[:, half(h)], E[2 + h][:, 0:H], ACT.Identity, bias=b_col).then_inc(act_fT_hi, 1)
            act.wait_ge(dve_half_sign, 1)
            act.activation(gate_abs[:, 0], O[0][0:B, 0:D], ACT.Abs, scale=2.0).then_inc(act_gate_abs, 1)
            act.activation(gate_abs[:, 1], O[0][0:B, D:2 * D], ACT.Abs).then_inc(act_gate_abs, 1)
            for h in range(2):
                act.wait_ge(dve_fT_lo0, h + 1)
                act.activation(fT[:, half(h)], E[2 + h][:, 0:H], ACT.Identity, bias=b_col).then_inc(act_fT, 1)
            act.wait_ge(pe_gate0, 1)
            act.copy(gates[:, 0].rearrange("p g d -> p (g d)"), O[0][:, 2 * D:4 * D]).then_inc(act_gate0, 1)

            def scaled_h2T(b):
                act.wait_ge(pe_h2T, b + 1)
                at_least(act, dve_xr, b)
                modulate(h2T[:, 1:S + 1], h2T_bank(b)[:], b, 2, act_h2T)

            for t in STEPS:
                if is_mixed(t - 2) and t < LAST:
                    tanh(t - 2, slice(0, S), r_bank(t - 2)[:])
                if t == 0:
                    act.wait_ge(pe_wT, 1)
                    act.copy(ffn_wT[:], C[:, 0:3 * P].rearrange("p (n d) -> p n d", n=3)).then_inc(act_wT, 1)
                if 0 <= t:
                    act.wait_ge(pe_nmx, t + 1)
                    act.copy(nmx_row[:], O[0][0:2, :]).then_inc(act_nmx, 1)
                if t == LAST:
                    tanh(t - 2, slice(0, S), r_bank(t - 2)[:])
                    scaled_h2T(t - 1)
                if 0 < t + 1 < B:
                    act.wait_ge(pe_xnT, t + 3)
                    act.wait_ge(pe_fT, t + 2)
                    modulate(hT[:], O[1][:], t + 1, 0, act_hT)
                if 0 <= t:
                    at_least(act, pe_pv, 2 * t)
                    exp(t, 0)
                    exp(t, 1)
                if is_mixed(t - 1) and t < LAST:
                    scaled_h2T(t - 1)
                if 0 <= t:
                    exp(t, 2)
                    exp(t, 3)
                if 0 < t + 1 < B:
                    act.wait_ge(pe_fT, t + 3)
                    act.wait_ge(pe_ftok, t + 1)
                    if t == 0:
                        act.wait_ge(dve_fT_lo0, 2)
                    at_least(act, pool_fT_lo, t)
                    f_parts(fT[:], fT_hi[:], A[:])
                if t + 2 < B:
                    act.wait_ge(pool_sh1, t + 2)
                    act.wait_ge(pe_xnT, t + 3)
                    normalize(xn, t + 2, range(NT), rstd1, sh1, act_xn)
                if is_mixed(t - 1):
                    squared_relu(t - 1, slice(0, S), kv_bank(t - 1)[:])
                if 0 <= t < LAST:
                    at_least(act, pe_h2T, t)
                    for h in range(2):
                        act.wait_ge(pool_sh2, 2 * t + h + 1)
                        normalize(xn2, t, blocks(h), rstd2, sh2, act_xn2)
            act.wait_ge(dve_xr, LAST)
            for h in range(2):
                if h == 0:
                    tanh(LAST - 1, slice(0, S), r_bank(LAST - 1)[:])
                act.wait_ge(pe_h2T, LAST + h + 1)
                modulate(h2T[:, 1 + h * H:1 + (h + 1) * H], E[h][:, 0:H], LAST, 2, act_h2T)
            for h in range(2):
                squared_relu(LAST + h, half(h), O[h][:, 0:H])
                tanh(LAST + h, half(h), E[h][:, 0:H])

        @block.vector
        def _(dve):
            dve.memset(neg_half[:], -0.5).then_inc(dve_const, 1)
            dve.memset(h2T[:, 0:1], 0.0).then_inc(dve_const, 1)
            dve.memset(ones_r[:].bitcast(F32), 1.0).then_inc(dve_const, 1)
            dve.memset(one_row[:], 1.0).then_inc(dve_const, 1)
            dve.memset(ftok[:, :, D:D + 1], 1.0).then_inc(dve_const, 1)
            dve.wait_ge(pool_ident, 2)
            dve.tensor_copy(ident_r[:], ident[:]).then_inc(dve_const, 1)

            def block_stats(b, js, st, s_st):
                for j in js:
                    dve.bn_stats(st[:, j], xs[:, b, j]).then_inc(s_st, 1)

            def merged_stats(js, st, mv, s_st, s_mv, seen):
                for n, j in enumerate(js):
                    dve.wait_ge(s_st, seen + n + 1)
                    ins = dve.bn_aggr(mv[:, j], st[:, j])
                ins.then_inc(s_mv, 1)

            def stats(b, js, st, mv, s_st, s_mv, seen):
                block_stats(b, js, st, s_st)
                merged_stats(js, st, mv, s_st, s_mv, seen)

            def stats1(b):
                if b <= 3:
                    dve.wait_ge((x1_in, x2_in, x_rest_in)[b - 1], 16 if b < 3 else 16 * (B - 3))
                dve.wait_ge(pool_ve1, 2 * b)
                dve.wait_ge(dve_mv1, b + 1)
                block_stats(b, range(NT), st1, dve_st1)
                if is_mixed(b - 4):
                    gated_v(b - 4, slice(0, S), kv_bank(b - 4)[:])
                merged_stats(range(NT), st1, mv1, dve_st1, dve_mv1, NT * b)

            def normalize(dst, b, h, mv, rs, s_rstd, n, done):
                dve.wait_ge(s_rstd, n + 1)
                for j in blocks(h):
                    ins = dve.tensor_scalar(dst[:, j], xs[:, b, j], mv[:, j, 0:1], rs[:, j:j + 1],
                                            ALU.subtract, ALU.mult)
                ins.then_inc(done, 1)

            def mixed_tokens(n, cols, prev):
                dve.wait_ge(act_h2T, n + 1)
                at_least(dve, dve_xr, n)
                nxt = slice(prev.start + 1, prev.stop + 1)
                dve.tensor_tensor(dT[:, cols], h2T[:, nxt], h2T[:, prev], ALU.subtract).then_inc(dve_d, 1)
                dve.wait_ge(dve_d, n + 1)
                at_least(dve, pe_k, min(n, LAST))
                dve.scalar_tensor_tensor(xkT[:, cols], dT[:, cols], mu_k_col, h2T[:, prev], ALU.mult,
                                         ALU.add).then_inc(dve_xk, 1)
                at_least(dve, pe_r, min(n, LAST))
                dve.scalar_tensor_tensor(xrT[:, cols], dT[:, cols], mu_r_col, h2T[:, prev], ALU.mult,
                                         ALU.add).then_inc(dve_xr, 1)

            def gated_v(n, cols, src):
                dve.wait_ge(pe_v, n + 1)
                dve.wait_ge(act_tanh, n + 1)
                if n < LAST:
                    at_least(dve, pool_y, n)
                dve.scalar_tensor_tensor((gv if n < LAST else last_gv)[:, cols],
                                         (th_r if n < LAST else last_th_r)[:, cols], 1.0, src, ALU.add,
                                         ALU.mult).then_inc(dve_gv, 1)

            dve.wait_ge(x0_in[0], 16)
            stats(0, blocks(0), st1, mv1, dve_st1, dve_mv1, 0)
            dve.wait_ge(act_cT, 1)
            dve.scalar_tensor_tensor(silu2[:], th_c[:], 1.0, A[:, 0:B], ALU.add, ALU.mult).then_inc(dve_silu, 1)
            dve.wait_ge(dve_silu, 1)
            dve.tensor_scalar(silu[:], silu2[:], 0.5, None, ALU.mult).then_inc(dve_silu, 1)
            dve.wait_ge(x0_in[1], 16)
            stats(0, blocks(1), st1, mv1, dve_st1, dve_mv1, 2)
            normalize(xn, 0, 0, mv1, rstd1, pool_rstd1, 0, dve_xn0)
            md = O[1][:, 0:4 * B].rearrange("p (m b) -> p b m", m=4)

            def modulation(m):
                dve.wait_ge(pe_mod, m // 2 + 1)
                dve.tensor_copy(modT[:, :, m:m + 1], md[:, :, m:m + 1])
                dve.tensor_scalar(modT[:, :, m + 1:m + 2], md[:, :, m + 1:m + 2], 1.0, None, ALU.add).then_inc(dve_mod, 1)

            modulation(0)
            normalize(xn, 0, 1, mv1, rstd1, pool_rstd1, 1, dve_xn0)
            dve.wait_ge(act_absd, 1)
            dve.tensor_scalar(bias[:], absd[:], float(MAX_DISTANCE), SCALE, ALU.min, ALU.mult).then_inc(dve_bias, 1)
            stats1(1)
            for h in range(2):
                dve.wait_ge(act_fT_hi, h + 1)
                dve.scalar_tensor_tensor(fT_lo[:, half(h)], E[2 + h][:, 0:H], b_col, fT_hi[:, half(h)].bitcast(F32),
                                         ALU.add, ALU.subtract).then_inc(dve_fT_lo0, 1)
            dve.wait_ge(pe_gate, 1)
            dve.tensor_scalar(half_sign[:], O[0][0:B, 0:2 * D].rearrange("b (g d) -> b g d", g=2), 0.0, 0.5,
                              ALU.is_ge, ALU.subtract).then_inc(dve_half_sign, 1)
            dve.wait_ge(dve_half_sign, 1)
            for g in range(2):
                dve.wait_ge(act_gate_abs, g + 1)
                dve.scalar_tensor_tensor(gate[:, g], gate_abs[:, g], (2.0, 1.0)[g] * GATE_MIN, half_sign[:, g],
                                         ALU.max, ALU.mult).then_inc(dve_gate, 1)

            for t in STEPS:
                if 0 <= t:
                    at_least(dve, dve_nmx, t)
                    if t == 0:
                        dve.wait_ge(dve_bias, 1)
                    for i in range(NT):
                        if t == 0 and i == 2:
                            modulation(2)
                        dve.wait_ge(pe_scores, NT * t + i + 1)
                        dve.tensor_tensor_reduce(E[i][:], E[i][:], bias[:, (NT - 1 - i) * P:(NT - 1 - i) * P + S],
                                                 1.0, LOWEST, ALU.add, ALU.max, mx[:, i:i + 1]).then_inc(dve_max, 1)
                    dve.wait_ge(dve_max, NT * (t + 1))
                    at_least(dve, pe_nmx, t)
                    dve.tensor_scalar(nmx[:, :, 0], mx[:], -1.0, None, ALU.mult).then_inc(dve_nmx_hi, 1)
                    dve.wait_ge(dve_nmx_hi, t + 1)
                    dve.scalar_tensor_tensor(nmx[:, :, 1], mx[:], -1.0, nmx[:, :, 0].bitcast(F32), ALU.mult,
                                             ALU.subtract).then_inc(dve_nmx, 1)
                    if t == 0:
                        dve.wait_ge(act_gate0, 1)
                    if t == 1:
                        dve.wait_ge(gates_in, 16)
                    dve.wait_ge(pe_ftok, t + 1)
                    at_least(dve, pe_pv, 2 * t)
                    dve.tensor_tensor(ftok[:, :, 0:D], A[:].rearrange("p (j d) -> p j d", j=NT),
                                      gates[:, t, 0:1].to_broadcast([P, NT, D]), ALU.mult).then_inc(dve_ftok, 1)
                if 1 < t + 2 < B:
                    stats1(t + 2)
                if t == LAST:
                    mixed_tokens(t - 1, slice(0, S), slice(0, S))
                if is_mixed(t - 2) and t + 2 >= B:
                    gated_v(t - 2, slice(0, S), kv_bank(t - 2)[:])
                if is_mixed(t - 1) and t < LAST:
                    mixed_tokens(t - 1, slice(0, S), slice(0, S))
                if 0 <= t:
                    at_least(dve, dve_x1, NT * t)
                    at_least(dve, pool_ve2, 4 * t)
                    at_least(dve, dve_mv2, 2 * t)
                    for h in range(2):
                        ob = O[h][:, 0:2 * (D + 1)].rearrange("p (j d) -> p j d", j=2)
                        dve.wait_ge(pe_pv, 2 * t + h + 1)
                        dve.reciprocal(rl[:, 2 * h:2 * h + 2], ob[:, :, D]).then_inc(dve_rl, 1)
                        dve.wait_ge(dve_rl, 2 * t + h + 1)
                        for j in range(2):
                            n = 2 * h + j
                            dve.scalar_tensor_tensor(xs[:, t, n], ob[:, j, 0:D], rl[:, n:n + 1], xs[:, t, n],
                                                     ALU.mult, ALU.add).then_inc(dve_x1, 1)
                        dve.wait_ge(dve_x1, NT * t + 2 * h + 2)
                        stats(t, blocks(h), st2, mv2, dve_st2, dve_mv2, NT * t + 2 * h)
            normalize(xn2, LAST, 0, mv2, rstd2, pool_rstd2, 2 * LAST, dve_last_xn2)
            normalize(xn2, LAST, 1, mv2, rstd2, pool_rstd2, 2 * LAST + 1, dve_last_xn2)
            mixed_tokens(LAST, half(0), half(0))
            mixed_tokens(LAST + 1, half(1), half(1))
            gated_v(LAST - 1, slice(0, S), kv_bank(LAST - 1)[:])
            for h in range(2):
                gated_v(LAST + h, half(h), O[h][:, 0:H])
                dve.wait_ge(dve_gv, LAST + h + 1)
                dve.tensor_tensor(ys[:, LAST, 2 * h:2 * h + 2], xs[:, LAST, 2 * h:2 * h + 2],
                                  last_gv[:, half(h)].rearrange("p (j d) -> p j d", j=2), ALU.add).then_inc(dve_y, 1)

        @block.tensor
        def _(pe):
            def keep_warm(n):
                for _ in range(n):
                    pe.matmul(C[:, 0:P], ident[:], ident[:], start=True, stop=True)

            def each_block(js, dst, lhsT, rhs, done, transposed=False):
                for j in js:
                    if transposed:
                        mm = pe.transpose(dst(j), lhsT(j), rhs)
                    else:
                        mm = pe.matmul(dst(j), lhsT(j), rhs, start=True, stop=True)
                mm.then_inc(done, 1)

            pe.wait_ge(pool_ident, 2)
            keep_warm(WARM_C)
            pe.wait_ge(c_in, 16)
            pe.transpose(A[:, 0:B], c_sb[:], ident[0:B, 0:B]).then_inc(pe_cT, 1)
            keep_warm(WARM_MOD)
            wm6 = wm[:].rearrange("p (m d) -> p m d", m=6)

            def modulation(n, ms):
                for m in ms:
                    mm = pe.matmul(O[1][:, n * B:(n + 1) * B], wm6[:, m], silu[:], start=True, stop=True)
                    n += 1
                mm.then_inc(pe_mod, 1)

            pe.wait_ge(dve_silu, 2)
            pe.wait_ge(wmod_a_in, 16)
            modulation(0, (0, 1))
            pe.wait_ge(dve_xn0, 1)
            each_block(blocks(0), lambda j: E[0][:, blk(j)], lambda j: xn[:, j], ident[:], pe_xnT, True)
            pe.wait_ge(dve_xn0, 2)
            each_block(blocks(1), lambda j: E[1][:, blk(j % 2)], lambda j: xn[:, j], ident[:], pe_xnT, True)
            pe.wait_ge(wa_in, 32)
            for h in range(2):
                pe.wait_ge(act_hT, h + 1)
                pe.matmul(E[2 + h][:, 0:H], wa[:], hT[:, half(h)], start=True, stop=True).then_inc(pe_fT, 1)
            pe.wait_ge(wmod_in, 16)
            pe.matmul(O[0][0:B, 0:2 * D].rearrange("b (g d) -> b g d", g=2), silu[:], wm6[:, 2:6:3],
                      start=True, stop=True).then_inc(pe_gate, 1)

            def h2T_of(b):
                pe.wait_ge(act_xn2, 2 * b + 2)
                if b == 0:
                    pe.wait_ge(act_wT, 1)
                each_block(range(NT), lambda j: h2T_bank(b)[:, blk(j)], lambda j: xn2[:, j], ident[:], pe_h2T, True)

            def k_of(b):
                pe.wait_ge(dve_xk, b + 1)
                pe.wait_ge(act_h2T, b + 1)
                pe.matmul(kv_bank(b)[:], wkT, xkT[:], start=True, stop=True).then_inc(pe_k, 1)

            def v_of(b):
                pe.wait_ge(act_ka, b + 1)
                pe.wait_ge(pool_wv, b + 1)
                each_block(range(NT), lambda j: kv_bank(b)[:, blk(j)], lambda j: kaT[:, blk(j)], wv_g[:], pe_v)

            def r_of(b):
                pe.wait_ge(dve_xr, b + 1)
                each_block(range(NT), lambda j: r_bank(b)[:, blk(j)], lambda j: xrT[:, blk(j)], wrT, pe_r)

            def gates_of_batch_0():
                pe.wait_ge(dve_gate, 2)
                pe.matmul(O[0][:, 2 * D:4 * D], one_row[:], gate[0:1].rearrange("b g d -> b (g d)"), start=True,
                          stop=True).then_inc(pe_gate0, 1)

            for t in STEPS:
                if 0 <= t:
                    pe.wait_ge(act_fT_hi, t + 2)
                    for i in range(NT):
                        at_least(pe, act_exp, NT * (t - 1) + i + 1)
                        if t == 0 and i == 2:
                            pe.wait_ge(dve_mod, 1)
                            modulation(2, (3, 4))
                            gates_of_batch_0()
                            pe.wait_ge(act_fT, 2)
                        pe.matmul(E[i][:], fT_hi[:, blk(i)], fT_hi[:], start=True, stop=False)
                        if i == 0:
                            if t == 0:
                                pe.wait_ge(dve_fT_lo0, 2)
                            at_least(pe, pool_fT_lo, t)
                        pe.matmul(E[i][:], fT_lo[:, blk(i)], fT_hi[:], start=False, stop=False)
                        pe.matmul(E[i][:], fT_hi[:, blk(i)], fT_lo[:], start=False, stop=True).then_inc(pe_scores, 1)
                if is_mixed(t - 2):
                    pe.wait_ge(act_relu, t - 1)
                    r_of(t - 2)
                if 0 <= t:
                    each_block(range(NT), lambda j: A[:, blk(j)], lambda j: fT[:, blk(j)], ident[:], pe_ftok, True)
                    if t == 0:
                        pe.wait_ge(w_in, 80)
                        each_block(range(3), lambda n: C[:, blk(n)], lambda n: ffn_w[:, n], ident[:], pe_wT, True)
                        pe.wait_ge(act_gate0, 1)
                    if t == 1:
                        keep_warm(WARM_STEP_1)
                    pe.wait_ge(dve_nmx, t + 1)
                    at_least(pe, dve_x1, NT * t)
                    each_block(range(NT), lambda j: O[0][0:2, blk(j)].bitcast(F32R), lambda j: nmx[:, j],
                               ident_r[:], pe_nmx, True)
                if 0 < t + 1 < B:
                    pe.wait_ge(act_xn, t + 1)
                    each_block(range(NT), lambda j: O[1][:, blk(j)], lambda j: xn[:, j], ident[:], pe_xnT, True)
                if t == LAST:
                    h2T_of(t - 1)
                if is_mixed(t - 2) and t < LAST:
                    pe.wait_ge(act_tanh, t - 1)
                    v_of(t - 2)
                if 0 <= t:
                    pe.wait_ge(act_nmx, t + 1)
                    for i in range(NT):
                        pe.matmul(E[i][:], ones_r[:], nmx_row[:], start=False, stop=True,
                                  skip_group_check=True).then_inc(pe_shift, 1)
                if t == LAST:
                    pe.wait_ge(act_tanh, t - 1)
                    v_of(t - 2)
                if is_mixed(t - 1) and t < LAST:
                    at_least(pe, dve_gv, t - 1)
                    h2T_of(t - 1)
                if 0 < t + 1 < B:
                    pe.wait_ge(act_hT, t + 3)
                    pe.wait_ge(dve_ftok, t + 1)
                    pe.matmul(A[:], wa[:], hT[:], start=True, stop=True).then_inc(pe_fT, 1)
                if 0 <= t:
                    pe.wait_ge(dve_ftok, t + 1)
                    for h in range(2):
                        for k in range(NT):
                            if h == 0:
                                pe.wait_ge(act_exp, NT * t + k + 1)
                            for j in range(2):
                                mm = pe.matmul(O[h][:, j * (D + 1):(j + 1) * (D + 1)], pT[:, k, blk(2 * h + j)],
                                               ftok[:, k], start=(k == 0 and j == 0), stop=(k == NT - 1),
                                               skip_group_check=True)
                        mm.then_inc(pe_pv, 1)
                if is_mixed(t - 1) and t < LAST:
                    k_of(t - 1)

            def last_h2T(h):
                pe.wait_ge(dve_last_xn2, h + 1)
                each_block(blocks(h), lambda j: E[h][:, blk(j % 2)], lambda j: xn2[:, j], ident[:], pe_h2T, True)

            def last_k(h):
                pe.wait_ge(dve_xk, LAST + h + 1)
                pe.matmul(O[h][:, 0:H], wkT, xkT[:, half(h)], start=True, stop=True).then_inc(pe_k, 1)

            def last_r(h):
                pe.wait_ge(dve_xr, LAST + h + 1)
                pe.wait_ge(act_h2T, LAST + h + 1)
                each_block(blocks(h), lambda j: E[h][:, blk(j % 2)], lambda j: xrT[:, blk(j)], wrT, pe_r)

            def last_v(h):
                pe.wait_ge(act_ka, LAST + h + 1)
                pe.wait_ge(pool_wv, LAST + 1)
                each_block(blocks(h), lambda j: O[h][:, blk(j % 2)], lambda j: kaT[:, blk(j)], wv_g[:], pe_v)

            k_of(LAST - 1)
            r_of(LAST - 1)
            last_h2T(0)
            v_of(LAST - 1)
            keep_warm(WARM_LAST)
            last_h2T(1)
            keep_warm(WARM_LAST)
            last_k(0)
            last_r(0)
            keep_warm(WARM_LAST)
            last_k(1)
            last_v(0)
            last_r(1)
            last_v(1)


_INS = ["L0_attn_x", "L0_attn_W", "L0_attn_b", "L0_ffn_W_r", "L0_ffn_W_k", "L0_ffn_W_v", "L0_ffn_mu_r",
        "L0_ffn_mu_k", "L0_c", "L0_wmod"]
_OUTS = [((8, 512, 128), "float32")]


def kernel(**inputs):
    import numpy as _np
    import concourse.bacc as _bacc
    from concourse import mybir as _mybir
    from concourse.bass_utils import run_bass_kernel_spmd as _run

    nc = _bacc.Bacc("TRN2", target_bir_lowering=False, num_devices=1)
    arrays, args = {}, []
    for name in _INS:
        a = _np.ascontiguousarray(inputs[name])
        arrays[f"in_{name}_dram"] = a
        args.append(nc.dram_tensor(f"in_{name}_dram", a.shape, _mybir.dt.from_np(a.dtype), kind="ExternalInput").ap())
    for i, (shape, dtype) in enumerate(_OUTS):
        dt = _mybir.dt.from_np(_np.dtype(dtype))
        args.append(nc.dram_tensor(f"out_{i}_dram", shape, dt, kind="ExternalOutput").ap())
    adaln_attention_channelmix_kernel(nc, *args)
    r = _run(nc, [arrays], core_ids=[0])
    return r.results[0]["out_0_dram"]
```
